# Optimizing a Trainium2 kernel written in Bass

```python
import numpy as np
import jax
import jax.numpy as jnp

def _softmax(x, axis=-1):
    return jax.nn.softmax(x, axis=axis)

def _gelu(x):
    return jax.nn.gelu(x, approximate=True)

def _silu(x):
    return jax.nn.silu(x)

def _sigmoid(x):
    return jax.nn.sigmoid(x)

def _layernorm(x, axis=-1, eps=1e-05):
    m = jnp.mean(x, axis=axis, keepdims=True)
    v = jnp.var(x, axis=axis, keepdims=True)
    return (x - m) / jnp.sqrt(v + eps)

def _scatter_add(tgt, idx, src, axis=0):
    return tgt.at[idx].add(src)

def _segment_sum(src, seg, n):
    return jax.ops.segment_sum(src, seg, n)
kernel_name = 'mk_recurrent_d1_jaxref_r8_578c39'

def setup_inputs(seed: int=0):
    np.random.seed(seed)
    _w = jnp.asarray

    def _L0_attn_setup():
        import jax, jax.numpy as jnp
        import numpy as np
        EMB = 512
        HEADS = 32
        SCALE = 4
        D = EMB // HEADS
        HKV = HEADS // SCALE
        B, S = (2, 256)
        key = jax.random.key(seed)
        ks = jax.random.split(key, 7)
        std = 0.02
        return {'x': jax.random.normal(ks[0], (B, S, EMB), jnp.float32), 'Wq': jax.random.normal(ks[1], (EMB, D, HEADS), jnp.float32) * std, 'bq': jnp.zeros((D, HEADS), jnp.float32), 'Wk': jax.random.normal(ks[2], (EMB, D, HKV), jnp.float32) * std, 'bk': jnp.zeros((D, HKV), jnp.float32), 'Wv': jax.random.normal(ks[3], (EMB, D, HKV), jnp.float32) * std, 'bv': jnp.zeros((D, HKV), jnp.float32)}
    _L0_attn_in = _L0_attn_setup()

    def _L0_ffn_setup():
        import jax, jax.numpy as jnp
        import numpy as np
        RMS_EPS = 1e-05
        key = jax.random.key(seed)
        k1, k2, k3, k4 = jax.random.split(key, 4)
        B, S, H, I = (1, 256, 512, 1792)
        x = jax.random.normal(k1, (B, S, H), dtype=jnp.float32)
        ln_w = jnp.ones((H,), dtype=jnp.float32)
        gate_w = jax.random.normal(k2, (I, H), dtype=jnp.float32) * 0.02
        up_w = jax.random.normal(k3, (I, H), dtype=jnp.float32) * 0.02
        down_w = jax.random.normal(k4, (H, I), dtype=jnp.float32) * 0.02
        return {'x': x, 'ln_w': ln_w, 'gate_w': gate_w, 'up_w': up_w, 'down_w': down_w}
    _L0_ffn_in = _L0_ffn_setup()
    _d = {'L0_attn_x': _L0_attn_in['x'], 'L0_attn_Wq': _L0_attn_in['Wq'], 'L0_attn_bq': _L0_attn_in['bq'], 'L0_attn_Wk': _L0_attn_in['Wk'], 'L0_attn_bk': _L0_attn_in['bk'], 'L0_attn_Wv': _L0_attn_in['Wv'], 'L0_attn_bv': _L0_attn_in['bv'], 'L0_ffn_ln_w': _L0_ffn_in['ln_w'], 'L0_ffn_gate_w': _L0_ffn_in['gate_w'], 'L0_ffn_up_w': _L0_ffn_in['up_w'], 'L0_ffn_down_w': _L0_ffn_in['down_w']}
    _x0 = _d['L0_attn_x']
    _d['L0_attn_x'] = jax.random.normal(jax.random.fold_in(jax.random.key(seed), 1), (1, 2048, 512), dtype=_x0.dtype)
    del _x0
    return _d

def reference(L0_attn_x, L0_attn_Wq, L0_attn_bq, L0_attn_Wk, L0_attn_bk, L0_attn_Wv, L0_attn_bv, L0_ffn_ln_w, L0_ffn_gate_w, L0_ffn_up_w, L0_ffn_down_w):

    def _L0_attn_ref(x, Wq, bq, Wk, bk, Wv, bv):
        import jax, jax.numpy as jnp
        import numpy as np
        EMB = 512
        HEADS = 32
        SCALE = 4
        D = EMB // HEADS
        HKV = HEADS // SCALE
        B, S = (2, 256)
        q = jnp.einsum('bse,edh->bsdh', x, Wq) + bq
        k = jnp.einsum('bse,edh->bsdh', x, Wk) + bk
        v = jnp.einsum('bse,edh->bsdh', x, Wv) + bv
        k = jnp.repeat(k, SCALE, axis=-1)
        v = jnp.repeat(v, SCALE, axis=-1)
        scores = jnp.einsum('bsdh,bseh->bsde', q, k) / np.float32(np.sqrt(D))
        attn = jax.nn.softmax(scores, axis=-1)
        out = jnp.einsum('bsde,bseh->bsdh', attn, v)
        return out.reshape(x.shape[:-1] + (EMB,))

    def _L0_ffn_ref(x, ln_w, gate_w, up_w, down_w):
        import jax, jax.numpy as jnp
        import numpy as np
        RMS_EPS = 1e-05
        var = jnp.mean(jnp.square(x), axis=-1, keepdims=True)
        nx = x * jax.lax.rsqrt(var + RMS_EPS) * ln_w
        g = jnp.einsum('bsh,ih->bsi', nx, gate_w)
        u = jnp.einsum('bsh,ih->bsi', nx, up_w)
        return jnp.einsum('bsi,hi->bsh', jax.nn.silu(g) * u, down_w)
    x = L0_attn_x
    xn = _layernorm(x, axis=-1)
    s = _L0_attn_ref(xn, L0_attn_Wq, L0_attn_bq, L0_attn_Wk, L0_attn_bk, L0_attn_Wv, L0_attn_bv)
    g = _silu(_L0_ffn_ref(xn, L0_ffn_ln_w, L0_ffn_gate_w, L0_ffn_up_w, L0_ffn_down_w))
    x = x + s * g
    return x

_drawn_inputs = setup_inputs


def setup_inputs(seed=0):
    import zlib

    import numpy as np

    out = dict(_drawn_inputs(seed))
    spreads = {'L0_attn_bq': (0.0, 0.8),
     'L0_attn_bk': (0.0, 0.8),
     'L0_attn_bv': (0.0, 0.8),
     'L0_ffn_ln_w': (1.0, 0.6)}
    factors = {'L0_attn_Wq': 8.0,
     'L0_attn_Wk': 8.0,
     'L0_attn_Wv': 6.936,
     'L0_ffn_gate_w': 7.871,
     'L0_ffn_up_w': 6.824,
     'L0_ffn_down_w': 6.811}
    for name, (base, spread) in spreads.items():
        noise = np.random.default_rng([zlib.crc32(name.encode()), seed]).standard_normal(out[name].shape)
        drawn = base * np.exp(spread * noise) if base else spread * noise
        out[name] = jnp.asarray(drawn.astype(out[name].dtype))
    for name, factor in factors.items():
        out[name] = (out[name] * factor).astype(out[name].dtype)
    return out
```

```python
from contextlib import ExitStack

import concourse.bass as bass
from concourse import mybir

F32 = mybir.dt.float32
F32R = mybir.dt.float32r
ALU = mybir.AluOpType
ACT = mybir.ActivationFunctionType
X = mybir.AxisListType.X

P = 128
EPS = 1e-5
D = 16
HKV = 8
REP = 4
QKV = 3 * D * HKV
DG = D * HKV
HALF = D // 2


def build(nc, x, wq, bq, wk, bk, wv, bv, lnw, gate, up, down, out):
    T, E = x.shape
    K = E // P
    TILES = T // P
    TB = 512
    J = TB // P
    NB = T // TB
    NI = gate.shape[0]
    PHASES = 2
    S = NI // PHASES
    LAST = PHASES * NB - 1
    A = J // PHASES
    RAW = 2
    ATT = 13 * A
    TRANSPOSE_STEP = 3

    x_blocks = x.rearrange("(b j p) e -> b p j e", j=J, p=P)
    out_tiles = out.rearrange("(b j p) e -> b p j e", j=J, p=P)

    with ExitStack() as ctx:
        def sb(name, shape, dt=F32):
            return ctx.enter_context(nc.sbuf_tensor(name, shape, dt))

        def ps(name, shape):
            return ctx.enter_context(nc.psum_tensor(name, shape, F32))

        def sem(name):
            return ctx.enter_context(nc.semaphore(name))

        gate_hi, gate_lo = sb("gate_hi", [P, S, K, P], F32R), sb("gate_lo", [P, S, K, P], F32R)
        up_hi, up_lo = sb("up_hi", [P, S, K, P], F32R), sb("up_lo", [P, S, K, P], F32R)
        down_hi, down_lo = sb("down_hi", [P, S, E], F32R), sb("down_lo", [P, S, E], F32R)
        wqkv_hi, wqkv_lo = sb("wqkv_hi", [P, K, QKV], F32R), sb("wqkv_lo", [P, K, QKV], F32R)
        raw = sb("raw", [P, RAW * 3, E])
        fin = raw[:, 0:J, :]
        z = sb("z", [P, J, E])
        zT_raw = sb("zT_raw", [P, K, TB])
        zT_hi, zT_lo = sb("zT_hi", [P, K, TB], F32R), sb("zT_lo", [P, K, TB], F32R)
        h = sb("h", [P, 2, TB])
        h_hi, h_lo = sb("h_hi", [P, 2, TB], F32R), sb("h_lo", [P, 2, TB], F32R)
        y_part = sb("y_part", [P, TILES * E])
        attn = sb("attn", [P, TILES * DG])
        qkv = sb("qkv", [P, A, QKV])
        prod = sb("prod", [P, HALF * DG])
        scores = sb("scores", [P, A, D * D])
        row_max, row_sum = sb("row_max", [P, A, D]), sb("row_sum", [P, A, D])
        row_inv = sb("row_inv", [P, A, D])
        bias = sb("bias", [P, QKV])
        lnw_sb = sb("lnw_sb", [P, K])
        ident = sb("ident", [P, P])
        half = sb("half", [P, J])
        eps = sb("eps", [P, J])
        minus_half = sb("minus_half", [P, J])
        scratch = sb("scratch", [P, 2])
        stats = sb("stats", [P, J, 6])
        mean_var = sb("mean_var", [P, J, 2])
        tmp = sb("tmp", [P, 3, J])
        z_scale = sb("z_scale", [P, J])
        rms = sb("rms", [P, J])
        wq_raw = y_part[:, 0:K * E].rearrange("p (k n) -> p k n", k=K)
        wqkv_raw = y_part[:, K * E:K * (E + QKV)].rearrange("p (k n) -> p k n", k=K)
        bq_raw = y_part[:, 8 * E:9 * E]

        gate_ps = ps("gate_ps", [P, TB])
        up_ps = ps("up_ps", [P, 2, TB])
        y_ps = ps("y_ps", [P, J, E])
        aux_ps = ps("aux_ps", [P, 512])

        x_first = [sem(f"x_first{j}") for j in range(J)]
        x_loaded = sem("x_loaded")
        raw_loaded = [sem(f"raw_loaded{n}") for n in range(3 * RAW)]
        lnw_loaded, qkv_w_loaded, bias_loaded = sem("lnw_loaded"), sem("qkv_w_loaded"), sem("bias_loaded")
        fin_x_loaded, fin_stored = sem("fin_x_loaded"), sem("fin_stored")
        gate_done, up_done, down_done = sem("gate_done"), sem("up_done"), sem("down_done")
        qkv_done, transposed = sem("qkv_done"), sem("transposed")
        silu_done, h_hi_done = sem("silu_done"), sem("h_hi_done")
        zT_raw_done, zT_hi_done = sem("zT_raw_done"), sem("zT_hi_done")
        w_hi_done, wqkv_hi_done = sem("w_hi_done"), sem("wqkv_hi_done")
        exp_done, y_gate_done = sem("exp_done"), sem("y_gate_done")
        h_done, h_lo_done, zT_lo_done = sem("h_done"), sem("h_lo_done"), sem("zT_lo_done")
        w_lo_done, wqkv_summed, wqkv_lo_done = sem("w_lo_done"), sem("wqkv_summed"), sem("wqkv_lo_done")
        bias_summed, qkv_in_sbuf = sem("bias_summed"), sem("qkv_in_sbuf")
        bn_done, stats_done, z_done = sem("bn_done"), sem("stats_done"), sem("z_done")
        attn_step, scores_done = sem("attn_step"), sem("scores_done")
        gated_done, fin_done = sem("gated_done"), sem("fin_done")
        y_free = sem("y_free")
        ident_zero, const_done, pool_step, scales_done = (
            sem("ident_zero"), sem("const_done"), sem("pool_step"), sem("scales_done"))

        def wait(eng, s, value):
            if not isinstance(value, int) or value > 0:
                eng.wait_ge(s, value)

        def slot_free(blk, i):
            return S * blk + i - 1 + (i == 0)

        block = ctx.enter_context(nc.Block())

        @block.sync
        def _(sp):
            for j in range(J):
                sp.dma_start(z[:, j, :], x_blocks[0, :, j, :]).then_inc(x_first[j], 16)

            def load_step(step, r):
                for n, w in enumerate((gate, up, down)):
                    wait(sp, w_lo_done, 3 * (step - RAW) + n + 1)
                    src = w[bass.ds(step, 1)].rearrange("a p n -> (a p) n")
                    sp.dma_start(raw[:, 3 * r + n, :], src).then_inc(raw_loaded[3 * r + n], 16)

            for r in range(RAW):
                load_step(r, r)
            with sp.Fori(1, NI // RAW) as turn:
                for r in range(RAW):
                    load_step(RAW * turn + r, r)

            def load_fin_x(n):
                wait(sp, w_lo_done, 3 * NI) if isinstance(n, int) else sp.wait_ge(fin_stored, 16 * J * n)
                src = x_blocks[bass.ds(n, 1)].rearrange("a p j e -> (a p) j e")
                sp.dma_start(fin, src).then_inc(fin_x_loaded, 16)

            def store(n):
                dst = out_tiles[bass.ds(n, 1)].rearrange("a p j e -> (a p) j e")
                for j in range(J):
                    sp.wait_ge(fin_done, J * n + j + 1)
                    sp.dma_start(dst[:, j, :], fin[:, j, :]).then_inc(fin_stored, 16)

            load_fin_x(0)
            store(0)
            with sp.Fori(1, NB) as n:
                load_fin_x(n)
                store(n)
            sp.wait_ge(fin_stored, 16 * TILES)

        @block.gpsimd
        def _(pool):
            pool.memset(ident[:], 0.0).then_inc(ident_zero, 1)
            pool.memset(half[:], 0.5).then_inc(const_done, 1)
            pool.memset(eps[:], EPS).then_inc(const_done, 1)
            pool.memset(minus_half[:], -0.5).then_inc(const_done, 1)
            pool.wait_ge(ident_zero, 1)
            pool.affine_select(out=ident[:], in_=ident[:], compare_op=ALU.not_equal, fill=1.0, base=0,
                               pattern=[[-1, P]], channel_multiplier=1).then_inc(const_done, 1)
            pool.wait_ge(const_done, 4)

            def scales(blk):
                STEPS = 7
                var = mean_var[:, :, 1]
                rstd, ms, r2 = tmp[:, 0, :], tmp[:, 1, :], tmp[:, 2, :]
                count = [STEPS * blk]

                def step(instruction):
                    count[0] = count[0] + 1
                    instruction.then_inc(pool_step, 1)
                    pool.wait_ge(pool_step, count[0])

                pool.wait_ge(stats_done, J * (blk + 1))
                step(pool.tensor_tensor(ms, var, eps[:], ALU.add))
                step(pool.tensor_tensor(rstd, ms, minus_half[:], ALU.pow))
                step(pool.tensor_tensor(ms, var, rstd, ALU.mult))
                step(pool.tensor_tensor(ms, ms, rstd, ALU.mult))
                step(pool.tensor_tensor(ms, ms, eps[:], ALU.add))
                step(pool.tensor_tensor(r2, ms, minus_half[:], ALU.pow))
                step(pool.tensor_tensor(rms[:], ms, half[:], ALU.pow))
                pool.tensor_tensor(z_scale[:], rstd, r2, ALU.mult).then_inc(scales_done, 1)

            def next_block(blk, source):
                pool.wait_ge(transposed, J * (blk + 1))
                src = x_blocks[bass.ds(source, 1)].rearrange("a p j e -> (a p) j e")
                pool.dma_start(z[:], src).then_inc(x_loaded, 16)
                scales(blk + 1)

            scales(0)
            with pool.Fori(0, NB - 1) as blk:
                next_block(blk, blk + 1)
            next_block(NB - 1, 0)
            with pool.Fori(NB, LAST) as blk:
                next_block(blk, blk - (NB - 1))

        @block.tensor
        def _(pe):
            def product(acc, pairs, start, stop):
                for n, (lhsT, rhs) in enumerate(pairs):
                    last = pe.matmul(acc, lhsT, rhs, start=start and n == 0,
                                     stop=stop and n == len(pairs) - 1)
                return last

            def expand(w_hi, w_lo, step, blk, first_step):
                pairs = []
                for k in range(K):
                    pairs += [(w_hi[:, step, k, :], zT_hi[:, k, :]), (w_hi[:, step, k, :], zT_lo[:, k, :]),
                              (w_lo[:, step, k, :], zT_hi[:, k, :])]
                return pairs

            def gate_product(blk, phase, i):
                pe.wait_ge(w_lo_done, 3 * (S * phase + i) + 1)
                wait(pe, silu_done, S * blk + i)
                pairs = expand(gate_hi, gate_lo, i, blk, i == 0)
                for k in range(K):
                    if i == 0:
                        pe.wait_ge(zT_hi_done, K * blk + k + 1)
                        pe.wait_ge(zT_lo_done, K * blk + k + 1)
                    last = product(gate_ps[:], pairs[3 * k:3 * k + 3], k == 0, k == K - 1)
                last.then_inc(gate_done, 1)

            def up_product(blk, phase, i):
                pe.wait_ge(w_lo_done, 3 * (S * phase + i) + 2)
                wait(pe, h_done, slot_free(blk, i))
                product(up_ps[:, i % 2, :], expand(up_hi, up_lo, i, blk, False), True, True).then_inc(up_done, 1)

            def down_product(blk, phase, i):
                pe.wait_ge(w_lo_done, 3 * (S * phase + i) + 3)
                pe.wait_ge(h_lo_done, S * blk + i + 1)
                if i == 0:
                    wait(pe, y_free, J * blk)
                for j in range(J):
                    t = slice(j * P, (j + 1) * P)
                    pairs = [(h_hi[:, i % 2, t], down_hi[:, i, :]), (h_hi[:, i % 2, t], down_lo[:, i, :]),
                             (h_lo[:, i % 2, t], down_hi[:, i, :])]
                    last = product(y_ps[:, j, :], pairs, i == 0, i == S - 1)
                last.then_inc(down_done, 1)

            def qkv_product(blk, phase, a):
                if a:
                    pe.wait_ge(qkv_in_sbuf, A * blk + a)
                t = slice((A * phase + a) * P, (A * phase + a + 1) * P)
                pairs = []
                for k in range(K):
                    pairs += [(zT_hi[:, k, t], wqkv_hi[:, k, :]), (zT_hi[:, k, t], wqkv_lo[:, k, :]),
                              (zT_lo[:, k, t], wqkv_hi[:, k, :])]
                product(aux_ps[:, 0:QKV], pairs, True, True).then_inc(qkv_done, 1)

            def transpose_tile(dst, blk, j):
                pe.wait_ge(z_done, J * blk + j + 1)
                for k in range(K):
                    last = pe.transpose(dst[:, k * P:(k + 1) * P], z[:, j, k * P:(k + 1) * P], ident[:])
                last.then_inc(transposed, 1)

            def transpose_next(blk, j):
                if j:
                    pe.wait_ge(zT_raw_done, J * (blk + 1) + j)
                else:
                    pe.wait_ge(qkv_in_sbuf, A * (blk + 1))
                transpose_tile(aux_ps, blk + 1, j)

            def one_block(blk, phase, last=False):
                for i in range(S):
                    gate_product(blk, phase, i)
                    if i == S - 1 and not last:
                        transpose_next(blk, J - 1)
                    up_product(blk, phase, i)
                    if i < A:
                        qkv_product(blk, phase, i)
                    if TRANSPOSE_STEP <= i < S - 1 and not last:
                        transpose_next(blk, i - TRANSPOSE_STEP)
                    if i:
                        down_product(blk, phase, i - 1)
                down_product(blk, phase, S - 1)

            pe.wait_ge(const_done, 4)
            for j in range(J):
                transpose_tile(y_ps[:, j, :], 0, j)
            pe.wait_ge(wqkv_lo_done, 1)
            one_block(0, 0)
            with pe.Fori(1, NB) as blk:
                one_block(blk, 0)
            with pe.Fori(NB, LAST) as blk:
                one_block(blk, 1)
            one_block(LAST, 1, last=True)

        @block.scalar
        def _(act):
            act.dma_start(lnw_sb[:], lnw).then_inc(lnw_loaded, 16)
            act.dma_start(wq_raw, wq.rearrange("(k p) n -> p k n", p=P)).then_inc(qkv_w_loaded, 16)
            act.dma_start(wqkv_raw[:, :, DG:2 * DG], wk.rearrange("(k p) n -> p k n", p=P)).then_inc(qkv_w_loaded, 16)
            act.dma_start(wqkv_raw[:, :, 2 * DG:], wv.rearrange("(k p) n -> p k n", p=P)).then_inc(qkv_w_loaded, 16)
            act.dma_start(bq_raw, bq.partition_broadcast(P)).then_inc(bias_loaded, 16)
            act.dma_start(bias[:, DG:2 * DG], bk.partition_broadcast(P)).then_inc(bias_loaded, 16)
            act.dma_start(bias[:, 2 * DG:], bv.partition_broadcast(P)).then_inc(bias_loaded, 16)

            def weights_hi(phase, i):
                step = S * phase + i
                for n, w_hi in enumerate((gate_hi, up_hi, down_hi)):
                    slot = 3 * (step % RAW) + n
                    act.wait_ge(raw_loaded[slot], 16 * (step // RAW + 1))
                    if n < 2:
                        for k in range(K):
                            last = act.activation(w_hi[:, i, k, :], raw[:, slot, k * P:(k + 1) * P], ACT.Copy,
                                                  scale=lnw_sb[:, k:k + 1])
                    else:
                        last = act.activation(w_hi[:, i, :], raw[:, slot, :], ACT.Copy)
                    last.then_inc(w_hi_done, 1)

            def zT_raw_tile(src, blk, j):
                act.wait_ge(transposed, J * blk + j + 1)
                if j == 0:
                    wait(act, zT_lo_done, K * blk)
                act.activation(zT_raw[:, :, j * P:(j + 1) * P], src.rearrange("p (k t) -> p k t", k=K),
                               ACT.Copy).then_inc(zT_raw_done, 1)

            def zT_hi_chunk(k):
                act.activation(zT_hi[:, k, :], zT_raw[:, k, :], ACT.Copy).then_inc(zT_hi_done, 1)

            def h_hi_part(blk, i):
                act.wait_ge(h_done, S * blk + i + 1)
                wait(act, down_done, slot_free(blk, i))
                act.activation(h_hi[:, i % 2, :], h[:, i % 2, :], ACT.Copy).then_inc(h_hi_done, 1)

            def one_block(blk, phase, first=False, last=False, before=None):
                if before == 0:
                    act.wait_ge(down_done, S * blk)
                    for j in range(J):
                        act.activation(y_part[:, bass.ds((J * blk - J + j) * E, E)], y_ps[:, j, :],
                                       ACT.Copy).then_inc(y_free, 1)
                for i in range(S):
                    if first and i + 1 < S:
                        weights_hi(phase, i + 1)
                    wait(act, h_lo_done, slot_free(blk, i))
                    act.wait_ge(gate_done, S * blk + i + 1)
                    act.activation(h[:, i % 2, :], gate_ps[:], ACT.Silu).then_inc(silu_done, 1)
                    if i < S - 1 or last:
                        h_hi_part(blk, i)
                    else:
                        zT_raw_tile(aux_ps[:], blk + 1, J - 1)
                        act.wait_ge(up_done, S * (blk + 1))
                        act.wait_ge(zT_raw_done, J * (blk + 2))
                        zT_hi_chunk(0)
                        h_hi_part(blk, i)
                        for k in range(1, K):
                            zT_hi_chunk(k)
                    if i == 0 and before == 1:
                        y_gate(blk)
                    if TRANSPOSE_STEP <= i < S - 1 and not last:
                        zT_raw_tile(aux_ps[:], blk + 1, i - TRANSPOSE_STEP)
                    if i == 3:
                        act.wait_ge(scores_done, blk + 1)
                        act.activation(scores[:], scores[:], ACT.Exp, scale=float(D) ** -0.5).then_inc(exp_done, 1)

            def y_gate(blk):
                for j in range(J):
                    act.wait_ge(y_free, J * (blk - 1) + j + 1)
                    y = y_part[:, bass.ds((J * (blk - 1 - NB) + j) * E, E)]
                    act.activation(y, y, ACT.Silu).then_inc(y_gate_done, 1)

            act.wait_ge(lnw_loaded, 16)
            weights_hi(0, 0)
            for j in range(J):
                zT_raw_tile(y_ps[:, j, :], 0, j)
            act.wait_ge(zT_raw_done, J)
            for k in range(K):
                zT_hi_chunk(k)
            act.wait_ge(wqkv_summed, 1)
            act.wait_ge(qkv_w_loaded, 48)
            act.activation(wqkv_hi[:], wqkv_raw, ACT.Copy).then_inc(wqkv_hi_done, 1)
            one_block(0, 0, first=True)
            with act.Fori(1, NB) as blk:
                one_block(blk, 0, before=0)
            act.wait_ge(down_done, S * (NB - 1) + 1)
            weights_hi(1, 0)
            one_block(NB, 1, first=True, before=0)
            with act.Fori(NB + 1, LAST) as blk:
                one_block(blk, 1, before=1)
            one_block(LAST, 1, last=True, before=1)
            y_gate(LAST + 1)

        @block.vector
        def _(dve):
            def weights_lo(phase, i):
                step = S * phase + i
                for n, (w_hi, w_lo) in enumerate(((gate_hi, gate_lo), (up_hi, up_lo), (down_hi, down_lo))):
                    slot = 3 * (step % RAW) + n
                    dve.wait_ge(w_hi_done, 3 * step + n + 1)
                    if n < 2:
                        for k in range(K):
                            last = dve.scalar_tensor_tensor(
                                w_lo[:, i, k, :], raw[:, slot, k * P:(k + 1) * P], lnw_sb[:, k:k + 1],
                                w_hi[:, i, k, :].bitcast(F32), ALU.mult, ALU.subtract)
                    else:
                        last = dve.tensor_tensor(w_lo[:, i, :], raw[:, slot, :], w_hi[:, i, :].bitcast(F32),
                                                 ALU.subtract)
                    last.then_inc(w_lo_done, 1)

            def statistics(blk):
                for j in range(J):
                    if isinstance(blk, int) and blk == 0:
                        dve.wait_ge(x_first[j], 16)
                    elif j == 0:
                        dve.wait_ge(x_loaded, 16 * blk)
                    dve.bn_stats(stats[:, j, :], z[:, j, :]).then_inc(bn_done, 1)
                dve.wait_ge(bn_done, J * (blk + 1))
                dve.memset(scratch[:, 0:1], 0.0)
                for j in range(J):
                    dve.bn_aggr(mean_var[:, j, :], stats[:, j, :]).then_inc(stats_done, 1)

            def normalise(blk):
                dve.wait_ge(scales_done, blk + 1)
                for j in range(J):
                    dve.tensor_scalar(z[:, j, :], z[:, j, :], mean_var[:, j, 0:1], z_scale[:, j:j + 1],
                                      ALU.subtract, ALU.mult).then_inc(z_done, 1)

            def zT_lo_chunk(blk, k):
                dve.wait_ge(zT_hi_done, K * blk + k + 1)
                dve.tensor_tensor(zT_lo[:, k, :], zT_raw[:, k, :], zT_hi[:, k, :].bitcast(F32),
                                  ALU.subtract).then_inc(zT_lo_done, 1)

            def qkv_out(blk, phase, a):
                dve.wait_ge(qkv_done, A * blk + a + 1)
                j = A * phase + a
                dve.scalar_tensor_tensor(qkv[:, a, :], aux_ps[:, 0:QKV], rms[:, j:j + 1], bias[:],
                                         ALU.mult, ALU.add).then_inc(qkv_in_sbuf, 1)

            def attn_chain(blk, start):
                count = [ATT * blk + start]

                def step(instruction):
                    count[0] = count[0] + 1
                    instruction.then_inc(attn_step, 1)
                    dve.wait_ge(attn_step, count[0])
                return step

            def attn_scores(blk, a):
                step = attn_chain(blk, 6 * a)
                dve.wait_ge(qkv_in_sbuf, A * blk + a + 1)
                q = qkv[:, a, 0:DG].rearrange("p (d g) -> p d g", g=HKV)
                k = qkv[:, a, DG:2 * DG].rearrange("p (e g) -> p e g", g=HKV)
                pr = prod[:].rearrange("p (d e g) -> p d e g", e=D, g=HKV)
                s = scores[:, a, :].rearrange("p (d e) -> p d e", e=D)
                for d in (0, HALF):
                    step(dve.tensor_tensor(pr, q[:, d:d + HALF, :].unsqueeze(2).to_broadcast([P, HALF, D, HKV]),
                                           k.unsqueeze(1).to_broadcast([P, HALF, D, HKV]), ALU.mult))
                    step(dve.tensor_reduce(s[:, d:d + HALF, :], pr, X, ALU.add))
                step(dve.tensor_reduce(row_max[:, a, :], s, X, ALU.max))
                less = dve.tensor_tensor(s, s, row_max[:, a, :].unsqueeze(2).to_broadcast([P, D, D]), ALU.subtract)
                step(less)
                if a == A - 1:
                    dve.memset(scratch[:, 1:2], 0.0).then_inc(scores_done, 1)

            def attn_values(blk, tile, a):
                step = attn_chain(blk, 6 * A + 7 * a)
                dve.wait_ge(exp_done, blk + 1)
                e = scores[:, a, :].rearrange("p (d e) -> p d e", e=D)
                v = qkv[:, a, 2 * DG:].rearrange("p (g e) -> p g e", e=D)
                pr = prod[:].rearrange("p (d g e) -> p d g e", g=HKV, e=D)
                o = attn[:, bass.ds(tile * DG, DG)].rearrange("p (d g) -> p d g", g=HKV)
                for d in (0, HALF):
                    step(dve.tensor_tensor(pr, e[:, d:d + HALF, :].unsqueeze(2).to_broadcast([P, HALF, HKV, D]),
                                           v.unsqueeze(1).to_broadcast([P, HALF, HKV, D]), ALU.mult))
                    step(dve.tensor_reduce(o[:, d:d + HALF, :], pr, X, ALU.add))
                step(dve.tensor_reduce(row_sum[:, a, :], e, X, ALU.add))
                step(dve.reciprocal(row_inv[:, a, :], row_sum[:, a, :]))
                step(dve.tensor_tensor(o, o, row_inv[:, a, :].unsqueeze(2).to_broadcast([P, D, HKV]), ALU.mult))

            def y_sum(blk):
                dve.wait_ge(down_done, S * blk)
                for j in range(J):
                    y = y_part[:, bass.ds((J * (blk - 1 - NB) + j) * E, E)]
                    dve.tensor_tensor(y, y_ps[:, j, :], y, ALU.add).then_inc(y_free, 1)

            def finish(blk, j):
                n = blk - 1 - NB
                tile = J * n + j
                y = y_part[:, bass.ds(tile * E, E)]
                s = attn[:, bass.ds(tile * DG, DG)].unsqueeze(2).to_broadcast([P, DG, REP])
                y3 = y.rearrange("p (s r) -> p s r", r=REP)
                dve.wait_ge(y_gate_done, tile + 1)
                dve.tensor_tensor(y3, y3, s, ALU.mult).then_inc(gated_done, 1)
                if j == 0:
                    dve.wait_ge(fin_x_loaded, 16 * (n + 1))
                dve.wait_ge(gated_done, tile + 1)
                dve.tensor_tensor(fin[:, j, :], y, fin[:, j, :], ALU.add).then_inc(fin_done, 1)

            def one_block(blk, phase, first=False, last=False, before=None):
                if before == 1:
                    y_sum(blk)
                for i in range(S):
                    if first and i + 1 < S:
                        weights_lo(phase, i + 1)
                    dve.wait_ge(silu_done, S * blk + i + 1)
                    dve.wait_ge(up_done, S * blk + i + 1)
                    dve.tensor_tensor(h[:, i % 2, :], h[:, i % 2, :], up_ps[:, i % 2, :], ALU.mult)\
                       .then_inc(h_done, 1)
                    dve.wait_ge(h_hi_done, S * blk + i + 1)
                    dve.tensor_tensor(h_lo[:, i % 2, :], h[:, i % 2, :], h_hi[:, i % 2, :].bitcast(F32),
                                      ALU.subtract).then_inc(h_lo_done, 1)
                    tile = J * (blk - NB * phase) + A * phase
                    if i == 0:
                        qkv_out(blk, phase, 0)
                        attn_scores(blk, 0)
                    if i == 1:
                        qkv_out(blk, phase, 1)
                        if not last:
                            statistics(blk + 1)
                        if before == 1:
                            finish(blk, 0)
                    if i == 2:
                        if not last:
                            normalise(blk + 1)
                        attn_scores(blk, 1)
                    if i == 3 and before == 1:
                        for j in range(1, J):
                            finish(blk, j)
                    if i == 4:
                        attn_values(blk, tile, 0)
                    if i == 5:
                        attn_values(blk, tile + 1, 1)
                if not last:
                    for k in range(K):
                        zT_lo_chunk(blk + 1, k)

            statistics(0)
            dve.wait_ge(lnw_loaded, 16)
            weights_lo(0, 0)
            normalise(0)
            dve.wait_ge(qkv_w_loaded, 48)
            dve.tensor_reduce(wqkv_raw[:, :, 0:DG], wq_raw.rearrange("p k (n r) -> p k n r", r=REP), X,
                              ALU.add).then_inc(wqkv_summed, 1)
            dve.wait_ge(bias_loaded, 48)
            dve.tensor_reduce(bias[:, 0:DG], bq_raw.rearrange("p (n r) -> p n r", r=REP), X,
                              ALU.add).then_inc(bias_summed, 1)
            for k in range(K):
                zT_lo_chunk(0, k)
            dve.wait_ge(wqkv_hi_done, 1)
            dve.tensor_tensor(wqkv_lo[:], wqkv_raw, wqkv_hi[:].bitcast(F32), ALU.subtract)\
               .then_inc(wqkv_lo_done, 1)
            dve.wait_ge(bias_summed, 1)
            one_block(0, 0, first=True)
            with dve.Fori(1, NB) as blk:
                one_block(blk, 0)
            weights_lo(1, 0)
            one_block(NB, 1, first=True)
            with dve.Fori(NB + 1, LAST) as blk:
                one_block(blk, 1, before=1)
            one_block(LAST, 1, last=True, before=1)
            y_sum(LAST + 1)
            for j in range(J):
                finish(LAST + 1, j)


def kernel(L0_attn_x, L0_attn_Wq, L0_attn_bq, L0_attn_Wk, L0_attn_bk, L0_attn_Wv, L0_attn_bv,
           L0_ffn_ln_w, L0_ffn_gate_w, L0_ffn_up_w, L0_ffn_down_w):
    import numpy as np
    import concourse.bacc as bacc
    from concourse.bass_utils import run_bass_kernel_spmd

    _, T, E = L0_attn_x.shape
    I = L0_ffn_gate_w.shape[0]

    def expand(w):
        return np.asarray(w).reshape(I // P, P, E // P, P).transpose(0, 3, 2, 1).reshape(I // P, P, E)

    arrays = {
        "x": np.asarray(L0_attn_x).reshape(T, E),
        "wq": np.asarray(L0_attn_Wq).reshape(E, -1),
        "bq": np.asarray(L0_attn_bq).reshape(-1),
        "wk": np.asarray(L0_attn_Wk).reshape(E, -1),
        "bk": np.asarray(L0_attn_bk).reshape(-1),
        "wv": np.asarray(L0_attn_Wv).transpose(0, 2, 1).reshape(E, -1),
        "bv": np.asarray(L0_attn_bv).T.reshape(-1),
        "lnw": np.asarray(L0_ffn_ln_w).reshape(E // P, P).T,
        "gate": expand(L0_ffn_gate_w),
        "up": expand(L0_ffn_up_w),
        "down": np.asarray(L0_ffn_down_w).T.reshape(I // P, P, E),
    }
    arrays = {name: np.ascontiguousarray(a) for name, a in arrays.items()}
    nc = bacc.Bacc("TRN2", target_bir_lowering=False, num_devices=1)
    args = [nc.dram_tensor(name, a.shape, mybir.dt.from_np(a.dtype), kind="ExternalInput").ap()
            for name, a in arrays.items()]
    out = nc.dram_tensor("out", (T, E), F32, kind="ExternalOutput").ap()
    build(nc, *args, out)
    r = run_bass_kernel_spmd(nc, [arrays], core_ids=[0])
    return np.asarray(r.results[0]["out"]).reshape(1, T, E)
```

```python
from contextlib import ExitStack

import concourse.bass as bass
from concourse import mybir

F32 = mybir.dt.float32
F32R = mybir.dt.float32r
ALU = mybir.AluOpType
ACT = mybir.ActivationFunctionType
X = mybir.AxisListType.X

P = 128
EPS = 1e-5
D = 16
HKV = 8
REP = 4
QKV = 3 * D * HKV
DG = D * HKV
HALF = D // 2


def build(nc, x, wq, bq, wk, bk, wv, bv, lnw, gate, up, down, out):
    T, E = x.shape
    K = E // P
    TILES = T // P
    TB = 512
    J = TB // P
    NB = T // TB
    NI = gate.shape[0]
    PHASES = 2
    S = NI // PHASES
    LAST = PHASES * NB - 1
    A = J // PHASES
    RAW = 2
    ATT = 13 * A
    QKV_STEP = 1
    TRANSPOSE_STEP = QKV_STEP + A
    SCORES_STEP, EXP_STEP, VALUES_STEP = (3, 2), (4, 3), 4
    FINISH_STEPS = (2, 5)
    assert J == K and TRANSPOSE_STEP + J - 1 == S - 1

    x_blocks = x.rearrange("(b j p) e -> b p j e", j=J, p=P)
    out_tiles = out.rearrange("(b j p) e -> b p j e", j=J, p=P)

    zT_kept = nc.dram_tensor("zT_kept", [NB - 1, P, K * TB], F32).ap()

    with ExitStack() as ctx:
        def sb(name, shape, dt=F32):
            return ctx.enter_context(nc.sbuf_tensor(name, shape, dt))

        def ps(name, shape):
            return ctx.enter_context(nc.psum_tensor(name, shape, F32))

        def sem(name):
            return ctx.enter_context(nc.semaphore(name))

        gate_hi, gate_lo = sb("gate_hi", [P, S, K, P], F32R), sb("gate_lo", [P, S, K, P], F32R)
        up_hi, up_lo = sb("up_hi", [P, S, K, P], F32R), sb("up_lo", [P, S, K, P], F32R)
        down_hi, down_lo = sb("down_hi", [P, S, E], F32R), sb("down_lo", [P, S, E], F32R)
        wqkv_hi, wqkv_lo = sb("wqkv_hi", [P, K, QKV], F32R), sb("wqkv_lo", [P, K, QKV], F32R)
        raw = sb("raw", [P, RAW * 3, E])
        fin = raw[:, 0:J, :]
        z = sb("z", [P, J, E])
        zT_raw = sb("zT_raw", [P, K, TB])
        zT_hi, zT_lo = sb("zT_hi", [P, K, TB], F32R), sb("zT_lo", [P, K, TB], F32R)
        h = sb("h", [P, 2, TB])
        h_hi, h_lo = sb("h_hi", [P, 2, TB], F32R), sb("h_lo", [P, 2, TB], F32R)
        y_part = sb("y_part", [P, TILES * E])
        attn = sb("attn", [P, TILES * DG])
        qkv = sb("qkv", [P, A, QKV])
        prod = sb("prod", [P, HALF * DG])
        scores = sb("scores", [P, A, D * D])
        row_max, row_sum = sb("row_max", [P, A, D]), sb("row_sum", [P, A, D])
        row_inv = sb("row_inv", [P, A, D])
        bias = sb("bias", [P, QKV])
        lnw_sb = sb("lnw_sb", [P, K])
        ident = sb("ident", [P, P])
        half = sb("half", [P, J])
        minus_half = sb("minus_half", [P, J])
        scratch = sb("scratch", [P, 3])
        stats = sb("stats", [P, J, 6])
        mean_var = sb("mean_var", [P, J, 2])
        z_var, x_var = sb("z_var", [P, J]), sb("x_var", [P, J])
        z_std, x_rstd = sb("z_std", [P, J]), sb("x_rstd", [P, J])
        z_scale = sb("z_scale", [P, J])
        rms = sb("rms", [P, TILES])
        wq_raw = y_part[:, 0:K * E].rearrange("p (k n) -> p k n", k=K)
        wqkv_raw = y_part[:, K * E:K * (E + QKV)].rearrange("p (k n) -> p k n", k=K)
        bq_raw = y_part[:, 8 * E:9 * E]

        gate_ps = ps("gate_ps", [P, TB])
        up_ps = ps("up_ps", [P, 2, TB])
        y_ps = ps("y_ps", [P, J, E])
        aux_ps = ps("aux_ps", [P, 512])

        x_first = [sem(f"x_first{j}") for j in range(J)]
        x_loaded = sem("x_loaded")
        raw_loaded = [sem(f"raw_loaded{n}") for n in range(3 * RAW)]
        lnw_loaded, qkv_w_loaded, bias_loaded = sem("lnw_loaded"), sem("qkv_w_loaded"), sem("bias_loaded")
        zT_stored, zT_loaded = sem("zT_stored"), sem("zT_loaded")
        fin_x_loaded, fin_stored = sem("fin_x_loaded"), sem("fin_stored")
        gate_done, up_done, down_done = sem("gate_done"), sem("up_done"), sem("down_done")
        qkv_done, transposed = sem("qkv_done"), sem("transposed")
        silu_done, h_hi_done = sem("silu_done"), sem("h_hi_done")
        zT_raw_done, zT_hi_done = sem("zT_raw_done"), sem("zT_hi_done")
        w_scaled, w_hi_done, wqkv_hi_done = sem("w_scaled"), sem("w_hi_done"), sem("wqkv_hi_done")
        table_loaded = sem("table_loaded")
        exp_done, y_gate_done = sem("exp_done"), sem("y_gate_done")
        h_done, h_lo_done, zT_lo_done = sem("h_done"), sem("h_lo_done"), sem("zT_lo_done")
        w_lo_done, wqkv_summed, wqkv_lo_done = sem("w_lo_done"), sem("wqkv_summed"), sem("wqkv_lo_done")
        bias_summed, qkv_in_sbuf = sem("bias_summed"), sem("qkv_in_sbuf")
        bn_done, stats_done, z_done = sem("bn_done"), sem("stats_done"), sem("z_done")
        var_done, attn_step = sem("var_done"), sem("attn_step")
        gated_done, fin_done = sem("gated_done"), sem("fin_done")
        y_free = sem("y_free")
        ident_zero, const_done, pool_step = sem("ident_zero"), sem("const_done"), sem("pool_step")
        z_scale_done, rms_done = sem("z_scale_done"), sem("rms_done")

        def wait(eng, s, value):
            if not isinstance(value, int) or value > 0:
                eng.wait_ge(s, value)

        def slot_free(blk, i):
            return S * blk + i - 1 + (i == 0)

        def y_whole(blk, j):
            if isinstance(blk, int) and blk == LAST:
                return J * (S * blk + S - 2) + (2 * J if j == J - 1 else J + j)
            return J * (S * blk + S - 1) + j + 1

        block = ctx.enter_context(nc.Block())

        @block.sync
        def _(sp):
            for j in range(J):
                sp.dma_start(z[:, j, :], x_blocks[0, :, j, :]).then_inc(x_first[j], 16)

            def load_step(step, r):
                for n, w in enumerate((gate, up, down)):
                    wait(sp, w_lo_done, 3 * (step - RAW) + n + 1)
                    src = w[bass.ds(step, 1)].rearrange("a p n -> (a p) n")
                    sp.dma_start(raw[:, 3 * r + n, :], src).then_inc(raw_loaded[3 * r + n], 16)

            load_step(0, 0)
            sp.dma_start(wq_raw, wq.rearrange("(k p) n -> p k n", p=P)).then_inc(qkv_w_loaded, 16)
            sp.dma_start(wqkv_raw[:, :, DG:2 * DG], wk.rearrange("(k p) n -> p k n", p=P)).then_inc(qkv_w_loaded, 16)
            sp.dma_start(wqkv_raw[:, :, 2 * DG:], wv.rearrange("(k p) n -> p k n", p=P)).then_inc(qkv_w_loaded, 16)
            load_step(1, 1)
            sp.dma_start(bq_raw, bq.partition_broadcast(P)).then_inc(bias_loaded, 16)
            sp.dma_start(bias[:, DG:2 * DG], bk.partition_broadcast(P)).then_inc(bias_loaded, 16)
            sp.dma_start(bias[:, 2 * DG:], bv.partition_broadcast(P)).then_inc(bias_loaded, 16)
            with sp.Fori(1, NI // RAW) as turn:
                for r in range(RAW):
                    load_step(RAW * turn + r, r)

            def load_fin_x(n):
                wait(sp, w_lo_done, 3 * NI) if isinstance(n, int) else sp.wait_ge(fin_stored, 16 * J * n)
                src = x_blocks[bass.ds(n, 1)].rearrange("a p j e -> (a p) j e")
                sp.dma_start(fin, src).then_inc(fin_x_loaded, 16)

            def store(n):
                dst = out_tiles[bass.ds(n, 1)].rearrange("a p j e -> (a p) j e")
                for j in range(J):
                    sp.wait_ge(fin_done, J * n + j + 1)
                    sp.dma_start(dst[:, j, :], fin[:, j, :]).then_inc(fin_stored, 16)

            load_fin_x(0)
            store(0)
            with sp.Fori(1, NB) as n:
                load_fin_x(n)
                store(n)
            sp.wait_ge(fin_stored, 16 * TILES)

        @block.gpsimd
        def _(pool):
            pool.memset(ident[:], 0.0).then_inc(ident_zero, 1)
            pool.memset(half[:], 0.5).then_inc(const_done, 1)
            pool.memset(minus_half[:], -0.5).then_inc(const_done, 1)
            pool.wait_ge(ident_zero, 1)
            pool.affine_select(out=ident[:], in_=ident[:], compare_op=ALU.not_equal, fill=1.0, base=0,
                               pattern=[[-1, P]], channel_multiplier=1).then_inc(const_done, 1)
            pool.wait_ge(const_done, 3)

            def scales(blk, source):
                pool.wait_ge(var_done, 2 * (blk + 1))
                pool.tensor_tensor(z_scale[:], z_var[:], minus_half[:], ALU.pow).then_inc(z_scale_done, 1)
                pool.tensor_tensor(x_rstd[:], x_var[:], minus_half[:], ALU.pow).then_inc(pool_step, 1)
                pool.tensor_tensor(z_std[:], z_var[:], half[:], ALU.pow).then_inc(pool_step, 1)
                pool.wait_ge(pool_step, 2 * (blk + 1))
                pool.tensor_tensor(rms[:, bass.ds(source * J, J)], x_rstd[:], z_std[:], ALU.mult)\
                    .then_inc(rms_done, 1)

            def next_x(blk, source):
                pool.wait_ge(transposed, J * (blk + 1))
                src = x_blocks[bass.ds(source, 1)].rearrange("a p j e -> (a p) j e")
                pool.dma_start(z[:], src).then_inc(x_loaded, 16)

            def keep_zT(blk):
                pool.wait_ge(zT_raw_done, J * blk)
                dst = zT_kept[bass.ds(blk - 1, 1)].rearrange("a p n -> (a p) n")
                pool.dma_start(dst, zT_raw[:].rearrange("p k t -> p (k t)")).then_inc(zT_stored, 16)

            scales(0, 0)
            next_x(0, 1)
            scales(1, 1)
            with pool.Fori(1, NB - 1) as blk:
                next_x(blk, blk + 1)
                keep_zT(blk)
                scales(blk + 1, blk + 1)
            next_x(NB - 1, 0)
            keep_zT(NB - 1)
            scales(NB, 0)
            pool.wait_ge(zT_stored, 16 * (NB - 1))
            with pool.Fori(NB, LAST) as blk:
                pool.wait_ge(zT_lo_done, K * (blk + 1))
                src = zT_kept[bass.ds(blk - NB, 1)].rearrange("a p n -> (a p) n")
                pool.dma_start(zT_raw[:].rearrange("p k t -> p (k t)"), src).then_inc(zT_loaded, 16)

        @block.tensor
        def _(pe):
            def product(acc, pairs, start, stop):
                for n, (lhsT, rhs) in enumerate(pairs):
                    last = pe.matmul(acc, lhsT, rhs, start=start and n == 0,
                                     stop=stop and n == len(pairs) - 1)
                return last

            def expand(w_hi, w_lo, step, blk, first_step):
                pairs = []
                for k in range(K):
                    pairs += [(w_hi[:, step, k, :], zT_hi[:, k, :]), (w_hi[:, step, k, :], zT_lo[:, k, :]),
                              (w_lo[:, step, k, :], zT_hi[:, k, :])]
                return pairs

            def gate_product(blk, phase, i):
                pe.wait_ge(w_lo_done, 3 * (S * phase + i) + 1)
                wait(pe, silu_done, S * blk + i)
                pairs = expand(gate_hi, gate_lo, i, blk, i == 0)
                for k in range(K):
                    if i == 0:
                        ready = K * blk + k + 1 if not isinstance(blk, int) or blk else K
                        pe.wait_ge(zT_hi_done, ready)
                        pe.wait_ge(zT_lo_done, ready)
                    last = product(gate_ps[:], pairs[3 * k:3 * k + 3], k == 0, k == K - 1)
                last.then_inc(gate_done, 1)

            def up_product(blk, phase, i):
                pe.wait_ge(w_lo_done, 3 * (S * phase + i) + 2)
                wait(pe, h_done, slot_free(blk, i))
                product(up_ps[:, i % 2, :], expand(up_hi, up_lo, i, blk, False), True, True).then_inc(up_done, 1)

            def down_wait(blk, phase, i):
                pe.wait_ge(w_lo_done, 3 * (S * phase + i) + 3)
                pe.wait_ge(h_lo_done, S * blk + i + 1)
                if i == 0:
                    wait(pe, y_free, J * blk)

            def down_tile(i, j):
                t = slice(j * P, (j + 1) * P)
                pairs = [(h_hi[:, i % 2, t], down_hi[:, i, :]), (h_hi[:, i % 2, t], down_lo[:, i, :]),
                         (h_lo[:, i % 2, t], down_hi[:, i, :])]
                product(y_ps[:, j, :], pairs, i == 0, i == S - 1).then_inc(down_done, 1)

            def down_product(blk, phase, i):
                down_wait(blk, phase, i)
                for j in range(J):
                    down_tile(i, j)

            def qkv_product(blk, phase, a):
                if isinstance(blk, int) and blk == 0 and a == 0:
                    pe.wait_ge(wqkv_lo_done, 1)
                if a:
                    pe.wait_ge(qkv_in_sbuf, A * blk + a)
                t = slice((A * phase + a) * P, (A * phase + a + 1) * P)
                pairs = []
                for k in range(K):
                    pairs += [(zT_hi[:, k, t], wqkv_hi[:, k, :]), (zT_hi[:, k, t], wqkv_lo[:, k, :]),
                              (zT_lo[:, k, t], wqkv_hi[:, k, :])]
                product(aux_ps[:, 0:QKV], pairs, True, True).then_inc(qkv_done, 1)

            def transpose_tile(dst, blk, j):
                pe.wait_ge(z_done, J * blk + j + 1)
                for k in range(K):
                    last = pe.transpose(dst[:, k * P:(k + 1) * P], z[:, j, k * P:(k + 1) * P], ident[:])
                last.then_inc(transposed, 1)

            def transpose_next(blk, j):
                if j:
                    pe.wait_ge(zT_raw_done, J * blk + j)
                else:
                    pe.wait_ge(qkv_in_sbuf, A * (blk + 1))
                transpose_tile(aux_ps, blk + 1, j)

            def one_block(blk, phase, last=False):
                for i in range(S):
                    gate_product(blk, phase, i)
                    if i == S - 1 and phase == 0:
                        transpose_next(blk, J - 1)
                    up_product(blk, phase, i)
                    if QKV_STEP <= i < TRANSPOSE_STEP:
                        qkv_product(blk, phase, i - QKV_STEP)
                    if TRANSPOSE_STEP <= i < S - 1 and phase == 0:
                        transpose_next(blk, i - TRANSPOSE_STEP)
                    if i and not (last and i == S - 1):
                        down_product(blk, phase, i - 1)
                if not last:
                    down_product(blk, phase, S - 1)
                else:
                    down_wait(blk, phase, S - 2)
                    for j in range(J - 1):
                        down_tile(S - 2, j)
                    down_wait(blk, phase, S - 1)
                    for j in range(J - 1):
                        down_tile(S - 1, j)
                    down_tile(S - 2, J - 1)
                    down_tile(S - 1, J - 1)

            pe.wait_ge(const_done, 3)
            for j in range(J):
                transpose_tile(y_ps[:, j, :], 0, j)
            one_block(0, 0)
            with pe.Fori(1, NB) as blk:
                one_block(blk, 0)
            with pe.Fori(NB, LAST) as blk:
                one_block(blk, 1)
            one_block(LAST, 1, last=True)

        @block.scalar
        def _(act):
            act.dma_start(lnw_sb[:], lnw).then_inc(lnw_loaded, 16)

            def weights_hi(phase, i, pieces=range(3)):
                step = S * phase + i
                for n in pieces:
                    slot = 3 * (step % RAW) + n
                    act.wait_ge(raw_loaded[slot], 16 * (step // RAW + 1))
                    if n < 2:
                        for k in range(K):
                            part = raw[:, slot, k * P:(k + 1) * P]
                            last = act.activation(part, part, ACT.Copy, scale=lnw_sb[:, k:k + 1])
                        last.then_inc(w_scaled, 1)
                        act.wait_ge(w_scaled, 2 * step + n + 1)
                        w_hi = (gate_hi, up_hi)[n][:, i, :, :].rearrange("p k n -> p (k n)")
                    else:
                        w_hi = down_hi[:, i, :]
                    act.activation(w_hi, raw[:, slot, :], ACT.Copy).then_inc(w_hi_done, 1)

            def zT_raw_tile(blk, j):
                act.wait_ge(transposed, J * blk + j + 1)
                if j == 0:
                    act.wait_ge(zT_lo_done, K * blk)
                    wait(act, zT_stored, 16 * (blk - 1))
                act.activation(zT_raw[:, :, j * P:(j + 1) * P], aux_ps[:].rearrange("p (k t) -> p k t", k=K),
                               ACT.Copy).then_inc(zT_raw_done, 1)

            def zT_hi_chunk(k):
                act.activation(zT_hi[:, k, :], zT_raw[:, k, :], ACT.Copy).then_inc(zT_hi_done, 1)

            def h_hi_part(blk, i):
                act.wait_ge(h_done, S * blk + i + 1)
                wait(act, down_done, J * slot_free(blk, i))
                act.activation(h_hi[:, i % 2, :], h[:, i % 2, :], ACT.Copy).then_inc(h_hi_done, 1)

            def one_block(blk, phase, first=False, last=False, before=None):
                if before == 0:
                    for j in range(J):
                        act.wait_ge(down_done, y_whole(blk - 1, j))
                        act.activation(y_part[:, bass.ds((J * blk - J + j) * E, E)], y_ps[:, j, :],
                                       ACT.Copy).then_inc(y_free, 1)
                for i in range(S):
                    if first and i + 1 < S:
                        weights_hi(phase, i + 1, (0,))
                    wait(act, h_lo_done, slot_free(blk, i))
                    act.wait_ge(gate_done, S * blk + i + 1)
                    act.activation(h[:, i % 2, :], gate_ps[:], ACT.Silu).then_inc(silu_done, 1)
                    if first and i + 1 < S:
                        weights_hi(phase, i + 1, (1, 2))
                    if i < S - 1 or last:
                        h_hi_part(blk, i)
                    else:
                        if phase == 0:
                            zT_raw_tile(blk + 1, J - 1)
                            act.wait_ge(zT_raw_done, J * (blk + 1))
                        else:
                            act.wait_ge(zT_loaded, 16 * (blk + 1 - NB))
                        act.wait_ge(up_done, S * (blk + 1))
                        zT_hi_chunk(0)
                        h_hi_part(blk, i)
                        for k in range(1, K):
                            zT_hi_chunk(k)
                    if i == 0 and before is None:
                        act.wait_ge(wqkv_summed, 1)
                        act.wait_ge(qkv_w_loaded, 48)
                        act.activation(wqkv_hi[:], wqkv_raw, ACT.Copy).then_inc(wqkv_hi_done, 1)
                    if i == 0 and before == 1:
                        y_gate(blk)
                    if TRANSPOSE_STEP <= i < S - 1 and phase == 0:
                        zT_raw_tile(blk + 1, i - TRANSPOSE_STEP)
                    if i == EXP_STEP[last]:
                        act.wait_ge(attn_step, ATT * blk + 6 * A)
                        act.activation(scores[:], scores[:], ACT.Exp, scale=float(D) ** -0.5).then_inc(exp_done, 1)

            def y_gate(blk):
                for j in range(J):
                    act.wait_ge(y_free, J * (blk - 1) + j + 1)
                    y = y_part[:, bass.ds((J * (blk - 1 - NB) + j) * E, E)]
                    act.activation(y, y, ACT.Silu).then_inc(y_gate_done, 1)

            act.wait_ge(table_loaded, 1)
            act.activation(scratch[:, 1:2], scratch[:, 0:1], ACT.Silu).then_inc(table_loaded, 1)
            act.wait_ge(lnw_loaded, 16)
            weights_hi(0, 0, (0, 1))
            for j in range(J):
                act.wait_ge(transposed, j + 1)
                act.activation(zT_hi[:, :, j * P:(j + 1) * P], y_ps[:, j, :].rearrange("p (k t) -> p k t", k=K),
                               ACT.Copy).then_inc(zT_hi_done, 1)
            weights_hi(0, 0, (2,))
            one_block(0, 0, first=True)
            with act.Fori(1, NB) as blk:
                one_block(blk, 0, before=0)
            act.wait_ge(down_done, J * (S * (NB - 1) + 1))
            weights_hi(1, 0)
            one_block(NB, 1, first=True, before=0)
            with act.Fori(NB + 1, LAST) as blk:
                one_block(blk, 1, before=1)
            one_block(LAST, 1, last=True, before=1)
            y_gate(LAST + 1)

        @block.vector
        def _(dve):
            def weights_lo(phase, i, pieces=range(3)):
                step = S * phase + i
                for n in pieces:
                    slot = 3 * (step % RAW) + n
                    w_hi, w_lo = ((gate_hi, gate_lo), (up_hi, up_lo), (down_hi, down_lo))[n]
                    w_hi, w_lo = w_hi[:, i], w_lo[:, i]
                    if n < 2:
                        w_hi, w_lo = w_hi.rearrange("p k n -> p (k n)"), w_lo.rearrange("p k n -> p (k n)")
                    dve.wait_ge(w_hi_done, 3 * step + n + 1)
                    dve.tensor_tensor(w_lo, raw[:, slot, :], w_hi.bitcast(F32), ALU.subtract)\
                        .then_inc(w_lo_done, 1)

            def statistics(blk):
                for j in range(J):
                    if isinstance(blk, int) and blk == 0:
                        dve.wait_ge(x_first[j], 16)
                    elif j == 0:
                        dve.wait_ge(x_loaded, 16 * blk)
                    dve.bn_stats(stats[:, j, :], z[:, j, :]).then_inc(bn_done, 1)
                dve.wait_ge(bn_done, J * (blk + 1))
                dve.memset(scratch[:, 2:3], 0.0)
                for j in range(J):
                    dve.bn_aggr(mean_var[:, j, :], stats[:, j, :]).then_inc(stats_done, 1)
                wait(dve, rms_done, blk)
                dve.wait_ge(stats_done, J * (blk + 1))
                dve.tensor_scalar(z_var[:], mean_var[:, :, 1], 1.0 + EPS, EPS * EPS, ALU.mult, ALU.add)\
                    .then_inc(var_done, 1)
                dve.tensor_scalar(x_var[:], mean_var[:, :, 1], EPS, None, ALU.add).then_inc(var_done, 1)

            def normalise(blk):
                dve.wait_ge(z_scale_done, blk + 1)
                for j in range(J):
                    dve.tensor_scalar(z[:, j, :], z[:, j, :], mean_var[:, j, 0:1], z_scale[:, j:j + 1],
                                      ALU.subtract, ALU.mult).then_inc(z_done, 1)

            def zT_lo_chunk(blk, k):
                dve.wait_ge(zT_hi_done, K * blk + k + 1)
                dve.tensor_tensor(zT_lo[:, k, :], zT_raw[:, k, :], zT_hi[:, k, :].bitcast(F32),
                                  ALU.subtract).then_inc(zT_lo_done, 1)

            def qkv_out(blk, tile, a):
                dve.wait_ge(qkv_done, A * blk + a + 1)
                dve.scalar_tensor_tensor(qkv[:, a, :], aux_ps[:, 0:QKV], rms[:, bass.ds(tile, 1)], bias[:],
                                         ALU.mult, ALU.add).then_inc(qkv_in_sbuf, 1)

            def attn_chain(blk, start):
                count = [ATT * blk + start]

                def step(instruction):
                    count[0] = count[0] + 1
                    instruction.then_inc(attn_step, 1)
                    dve.wait_ge(attn_step, count[0])
                return step

            def attn_scores(blk, a):
                step = attn_chain(blk, 6 * a)
                dve.wait_ge(qkv_in_sbuf, A * blk + a + 1)
                q = qkv[:, a, 0:DG].rearrange("p (d g) -> p d g", g=HKV)
                k = qkv[:, a, DG:2 * DG].rearrange("p (e g) -> p e g", g=HKV)
                pr = prod[:].rearrange("p (d e g) -> p d e g", e=D, g=HKV)
                s = scores[:, a, :].rearrange("p (d e) -> p d e", e=D)
                for d in (0, HALF):
                    step(dve.tensor_tensor(pr, q[:, d:d + HALF, :].unsqueeze(2).to_broadcast([P, HALF, D, HKV]),
                                           k.unsqueeze(1).to_broadcast([P, HALF, D, HKV]), ALU.mult))
                    step(dve.tensor_reduce(s[:, d:d + HALF, :], pr, X, ALU.add))
                step(dve.tensor_reduce(row_max[:, a, :], s, X, ALU.max))
                step(dve.tensor_tensor(s, s, row_max[:, a, :].unsqueeze(2).to_broadcast([P, D, D]), ALU.subtract))

            def attn_values(blk, tile, a):
                step = attn_chain(blk, 6 * A + 7 * a)
                dve.wait_ge(exp_done, blk + 1)
                e = scores[:, a, :].rearrange("p (d e) -> p d e", e=D)
                v = qkv[:, a, 2 * DG:].rearrange("p (g e) -> p g e", e=D)
                pr = prod[:].rearrange("p (d g e) -> p d g e", g=HKV, e=D)
                o = attn[:, bass.ds(tile * DG, DG)].rearrange("p (d g) -> p d g", g=HKV)
                for d in (0, HALF):
                    step(dve.tensor_tensor(pr, e[:, d:d + HALF, :].unsqueeze(2).to_broadcast([P, HALF, HKV, D]),
                                           v.unsqueeze(1).to_broadcast([P, HALF, HKV, D]), ALU.mult))
                    step(dve.tensor_reduce(o[:, d:d + HALF, :], pr, X, ALU.add))
                step(dve.tensor_reduce(row_sum[:, a, :], e, X, ALU.add))
                step(dve.reciprocal(row_inv[:, a, :], row_sum[:, a, :]))
                step(dve.tensor_tensor(o, o, row_inv[:, a, :].unsqueeze(2).to_broadcast([P, D, HKV]), ALU.mult))

            def y_sum(blk, tiles=range(J)):
                for j in tiles:
                    dve.wait_ge(down_done, y_whole(blk - 1, j))
                    y = y_part[:, bass.ds((J * (blk - 1 - NB) + j) * E, E)]
                    dve.tensor_tensor(y, y_ps[:, j, :], y, ALU.add).then_inc(y_free, 1)

            def finish(blk, j):
                n = blk - 1 - NB
                tile = J * n + j
                y = y_part[:, bass.ds(tile * E, E)]
                s = attn[:, bass.ds(tile * DG, DG)].unsqueeze(2).to_broadcast([P, DG, REP])
                y3 = y.rearrange("p (s r) -> p s r", r=REP)
                dve.wait_ge(y_gate_done, tile + 1)
                dve.tensor_tensor(y3, y3, s, ALU.mult).then_inc(gated_done, 1)
                if j == 0:
                    dve.wait_ge(fin_x_loaded, 16 * (n + 1))
                dve.wait_ge(gated_done, tile + 1)
                dve.tensor_tensor(fin[:, j, :], y, fin[:, j, :], ALU.add).then_inc(fin_done, 1)

            def qkv_weights_lo():
                dve.wait_ge(bias_loaded, 48)
                dve.tensor_reduce(bias[:, 0:DG], bq_raw.rearrange("p (n r) -> p n r", r=REP), X,
                                  ALU.add).then_inc(bias_summed, 1)
                dve.wait_ge(wqkv_hi_done, 1)
                dve.tensor_tensor(wqkv_lo[:], wqkv_raw, wqkv_hi[:].bitcast(F32), ALU.subtract)\
                   .then_inc(wqkv_lo_done, 1)
                dve.wait_ge(bias_summed, 1)

            def one_block(blk, phase, first=False, last=False, before=None):
                if before == 1:
                    y_sum(blk)
                for i in range(S):
                    if first and i + 1 < S:
                        weights_lo(phase, i + 1, (0,))
                    dve.wait_ge(silu_done, S * blk + i + 1)
                    dve.wait_ge(up_done, S * blk + i + 1)
                    dve.tensor_tensor(h[:, i % 2, :], h[:, i % 2, :], up_ps[:, i % 2, :], ALU.mult)\
                       .then_inc(h_done, 1)
                    dve.wait_ge(h_hi_done, S * blk + i + 1)
                    dve.tensor_tensor(h_lo[:, i % 2, :], h[:, i % 2, :], h_hi[:, i % 2, :].bitcast(F32),
                                      ALU.subtract).then_inc(h_lo_done, 1)
                    if first and i + 1 < S:
                        weights_lo(phase, i + 1, (1, 2))
                    tile = J * (blk - NB * phase) + A * phase
                    if i == 0 and before is None:
                        qkv_weights_lo()
                    elif i == 0:
                        attn_values(blk - 1, J * (blk - 1 - NB * before) + A * before + 1, 1)
                    if i == 0 and phase == 0:
                        statistics(blk + 1)
                    if i == 1:
                        if phase == 0 or first:
                            dve.wait_ge(rms_done, blk + 1)
                        qkv_out(blk, tile, 0)
                        attn_scores(blk, 0)
                    if i == 2:
                        qkv_out(blk, tile + 1, 1)
                        if phase == 0:
                            normalise(blk + 1)
                    if i == SCORES_STEP[last]:
                        attn_scores(blk, 1)
                    if i in FINISH_STEPS and before == 1 and not last:
                        for j in range(J):
                            if FINISH_STEPS[j // 2] == i:
                                finish(blk, j)
                    if i == 3 and last:
                        for j in range(J):
                            finish(blk, j)
                    if i == VALUES_STEP:
                        attn_values(blk, tile, 0)
                    if i == S - 2 and last:
                        attn_values(blk, tile + 1, 1)
                if not last:
                    for k in range(K):
                        zT_lo_chunk(blk + 1, k)

            dve.memset(scratch[:, 0:1], 0.0).then_inc(table_loaded, 1)
            statistics(0)
            normalise(0)
            weights_lo(0, 0, (0,))
            for j in range(J):
                dve.wait_ge(zT_hi_done, j + 1)
                t = slice(j * P, (j + 1) * P)
                dve.tensor_tensor(zT_lo[:, :, t], y_ps[:, j, :].rearrange("p (k t) -> p k t", k=K),
                                  zT_hi[:, :, t].bitcast(F32), ALU.subtract).then_inc(zT_lo_done, 1)
            weights_lo(0, 0, (1, 2))
            dve.wait_ge(qkv_w_loaded, 48)
            dve.tensor_reduce(wqkv_raw[:, :, 0:DG], wq_raw.rearrange("p k (n r) -> p k n r", r=REP), X,
                              ALU.add).then_inc(wqkv_summed, 1)
            one_block(0, 0, first=True)
            with dve.Fori(1, NB) as blk:
                one_block(blk, 0, before=0)
            weights_lo(1, 0)
            one_block(NB, 1, first=True, before=0)
            with dve.Fori(NB + 1, LAST) as blk:
                one_block(blk, 1, before=1)
            one_block(LAST, 1, last=True, before=1)
            y_sum(LAST + 1, (0, 1))
            for j in range(J):
                finish(LAST + 1, j)
                if j + 2 < J:
                    y_sum(LAST + 1, (j + 2,))


def kernel(L0_attn_x, L0_attn_Wq, L0_attn_bq, L0_attn_Wk, L0_attn_bk, L0_attn_Wv, L0_attn_bv,
           L0_ffn_ln_w, L0_ffn_gate_w, L0_ffn_up_w, L0_ffn_down_w):
    import numpy as np
    import concourse.bacc as bacc
    from concourse.bass_utils import run_bass_kernel_spmd

    _, T, E = L0_attn_x.shape
    I = L0_ffn_gate_w.shape[0]

    def expand(w):
        return np.asarray(w).reshape(I // P, P, E // P, P).transpose(0, 3, 2, 1).reshape(I // P, P, E)

    arrays = {
        "x": np.asarray(L0_attn_x).reshape(T, E),
        "wq": np.asarray(L0_attn_Wq).reshape(E, -1),
        "bq": np.asarray(L0_attn_bq).reshape(-1),
        "wk": np.asarray(L0_attn_Wk).reshape(E, -1),
        "bk": np.asarray(L0_attn_bk).reshape(-1),
        "wv": np.asarray(L0_attn_Wv).transpose(0, 2, 1).reshape(E, -1),
        "bv": np.asarray(L0_attn_bv).T.reshape(-1),
        "lnw": np.asarray(L0_ffn_ln_w).reshape(E // P, P).T,
        "gate": expand(L0_ffn_gate_w),
        "up": expand(L0_ffn_up_w),
        "down": np.asarray(L0_ffn_down_w).T.reshape(I // P, P, E),
    }
    arrays = {name: np.ascontiguousarray(a) for name, a in arrays.items()}
    nc = bacc.Bacc("TRN2", target_bir_lowering=False, num_devices=1)
    args = [nc.dram_tensor(name, a.shape, mybir.dt.from_np(a.dtype), kind="ExternalInput").ap()
            for name, a in arrays.items()]
    out = nc.dram_tensor("out", (T, E), F32, kind="ExternalOutput").ap()
    build(nc, *args, out)
    r = run_bass_kernel_spmd(nc, [arrays], core_ids=[0])
    return np.asarray(r.results[0]["out"]).reshape(1, T, E)
```

```python
from contextlib import ExitStack

import concourse.bass as bass
from concourse import mybir

F32 = mybir.dt.float32
F32R = mybir.dt.float32r
ALU = mybir.AluOpType
ACT = mybir.ActivationFunctionType
X = mybir.AxisListType.X

P = 128
EPS = 1e-5
D = 16
HKV = 8
REP = 4
QKV = 3 * D * HKV
DG = D * HKV
HALF = D // 2


def build(nc, x, wq, bq, wk, bk, wv, bv, lnw, gate, up, down, out):
    T, E = x.shape
    K = E // P
    TILES = T // P
    TB = 512
    J = TB // P
    NB = T // TB
    NI = gate.shape[0]
    PHASES = 2
    S = NI // PHASES
    LAST = PHASES * NB - 1
    A = J // PHASES
    WARM_UP = 32
    RAW = 2
    ATT = 13 * A
    QKV_STEP = 1
    TRANSPOSE_STEP = QKV_STEP + A
    SCORES_STEP, EXP_STEP, VALUES_STEP = (3, 2), (4, 3), 4
    FINISH_STEPS = (2, 5)
    assert J == K and TRANSPOSE_STEP + J - 1 == S - 1

    x_blocks = x.rearrange("(b j p) e -> b p j e", j=J, p=P)
    out_tiles = out.rearrange("(b j p) e -> b p j e", j=J, p=P)

    zT_kept = nc.dram_tensor("zT_kept", [NB - 1, P, K * TB], F32).ap()

    with ExitStack() as ctx:
        def sb(name, shape, dt=F32):
            return ctx.enter_context(nc.sbuf_tensor(name, shape, dt))

        def ps(name, shape):
            return ctx.enter_context(nc.psum_tensor(name, shape, F32))

        def sem(name):
            return ctx.enter_context(nc.semaphore(name))

        gate_hi, gate_lo = sb("gate_hi", [P, S, K, P], F32R), sb("gate_lo", [P, S, K, P], F32R)
        up_hi, up_lo = sb("up_hi", [P, S, K, P], F32R), sb("up_lo", [P, S, K, P], F32R)
        down_hi, down_lo = sb("down_hi", [P, S, E], F32R), sb("down_lo", [P, S, E], F32R)
        wqkv_hi, wqkv_lo = sb("wqkv_hi", [P, K, QKV], F32R), sb("wqkv_lo", [P, K, QKV], F32R)
        raw = sb("raw", [P, RAW * 3, E])
        fin = raw[:, 0:J, :]
        z = sb("z", [P, J, E])
        zT_raw = sb("zT_raw", [P, K, TB])
        zT_hi, zT_lo = sb("zT_hi", [P, K, TB], F32R), sb("zT_lo", [P, K, TB], F32R)
        h = sb("h", [P, 2, TB])
        h_hi, h_lo = sb("h_hi", [P, 2, TB], F32R), sb("h_lo", [P, 2, TB], F32R)
        y_part = sb("y_part", [P, TILES * E])
        attn = sb("attn", [P, TILES * DG])
        qkv = sb("qkv", [P, A, QKV])
        prod = sb("prod", [P, HALF * DG])
        scores = sb("scores", [P, A, D * D])
        row_max, row_sum = sb("row_max", [P, A, D]), sb("row_sum", [P, A, D])
        row_inv = sb("row_inv", [P, A, D])
        bias = sb("bias", [P, QKV])
        lnw_sb = sb("lnw_sb", [P, K])
        ident = sb("ident", [P, P])
        half = sb("half", [P, J])
        minus_half = sb("minus_half", [P, J])
        scratch = sb("scratch", [P, 3])
        stats = sb("stats", [P, J, 6])
        mean_var = sb("mean_var", [P, J, 2])
        z_var, x_var = sb("z_var", [P, J]), sb("x_var", [P, J])
        z_std, x_rstd = sb("z_std", [P, J]), sb("x_rstd", [P, J])
        z_scale = sb("z_scale", [P, J])
        rms = sb("rms", [P, TILES])
        wq_raw = y_part[:, 0:K * E].rearrange("p (k n) -> p k n", k=K)
        wqkv_raw = y_part[:, K * E:K * (E + QKV)].rearrange("p (k n) -> p k n", k=K)
        bq_raw = y_part[:, 8 * E:9 * E]

        gate_ps = ps("gate_ps", [P, TB])
        up_ps = ps("up_ps", [P, 2, TB])
        y_ps = ps("y_ps", [P, J, E])
        aux_ps = ps("aux_ps", [P, 512])

        x_first = [sem(f"x_first{j}") for j in range(J)]
        x_loaded = sem("x_loaded")
        raw_loaded = [sem(f"raw_loaded{n}") for n in range(3 * RAW)]
        lnw_loaded, qkv_w_loaded, bias_loaded = sem("lnw_loaded"), sem("qkv_w_loaded"), sem("bias_loaded")
        zT_stored, zT_loaded = sem("zT_stored"), sem("zT_loaded")
        fin_x_loaded, fin_stored = sem("fin_x_loaded"), sem("fin_stored")
        gate_done, up_done, down_done = sem("gate_done"), sem("up_done"), sem("down_done")
        qkv_done, transposed = sem("qkv_done"), sem("transposed")
        silu_done, h_hi_done = sem("silu_done"), sem("h_hi_done")
        zT_raw_done, zT_hi_done = sem("zT_raw_done"), sem("zT_hi_done")
        w_scaled, w_hi_done, wqkv_hi_done = sem("w_scaled"), sem("w_hi_done"), sem("wqkv_hi_done")
        table_loaded = sem("table_loaded")
        exp_done, y_gate_done = sem("exp_done"), sem("y_gate_done")
        h_done, h_lo_done, zT_lo_done = sem("h_done"), sem("h_lo_done"), sem("zT_lo_done")
        w_lo_done, wqkv_summed, wqkv_lo_done = sem("w_lo_done"), sem("wqkv_summed"), sem("wqkv_lo_done")
        bias_summed, qkv_in_sbuf = sem("bias_summed"), sem("qkv_in_sbuf")
        bn_done, stats_done, z_done = sem("bn_done"), sem("stats_done"), sem("z_done")
        var_done, attn_step = sem("var_done"), sem("attn_step")
        gated_done, fin_done = sem("gated_done"), sem("fin_done")
        y_free = sem("y_free")
        ident_zero, const_done, pool_step = sem("ident_zero"), sem("const_done"), sem("pool_step")
        z_scale_done, rms_done = sem("z_scale_done"), sem("rms_done")

        def wait(eng, s, value):
            if not isinstance(value, int) or value > 0:
                eng.wait_ge(s, value)

        def slot_free(blk, i):
            return S * blk + i - 1 + (i == 0)

        def y_whole(blk, j):
            if isinstance(blk, int) and blk == LAST:
                return J * (S * blk + S - 2) + (2 * J if j == J - 1 else J + j)
            return J * (S * blk + S - 1) + j + 1

        block = ctx.enter_context(nc.Block())

        @block.sync
        def _(sp):
            for j in range(J):
                sp.dma_start(z[:, j, :], x_blocks[0, :, j, :]).then_inc(x_first[j], 16)
            sp.dma_start(lnw_sb[:], lnw).then_inc(lnw_loaded, 16)

            def load_step(step, r):
                for n, w in enumerate((gate, up, down)):
                    wait(sp, w_lo_done, 3 * (step - RAW) + n + 1)
                    src = w[bass.ds(step, 1)].rearrange("a p n -> (a p) n")
                    sp.dma_start(raw[:, 3 * r + n, :], src).then_inc(raw_loaded[3 * r + n], 16)

            load_step(0, 0)
            sp.dma_start(wq_raw, wq.rearrange("(k p) n -> p k n", p=P)).then_inc(qkv_w_loaded, 16)
            sp.dma_start(wqkv_raw[:, :, DG:2 * DG], wk.rearrange("(k p) n -> p k n", p=P)).then_inc(qkv_w_loaded, 16)
            sp.dma_start(wqkv_raw[:, :, 2 * DG:], wv.rearrange("(k p) n -> p k n", p=P)).then_inc(qkv_w_loaded, 16)
            load_step(1, 1)
            sp.dma_start(bq_raw, bq.partition_broadcast(P)).then_inc(bias_loaded, 16)
            sp.dma_start(bias[:, DG:2 * DG], bk.partition_broadcast(P)).then_inc(bias_loaded, 16)
            sp.dma_start(bias[:, 2 * DG:], bv.partition_broadcast(P)).then_inc(bias_loaded, 16)
            with sp.Fori(1, NI // RAW) as turn:
                for r in range(RAW):
                    load_step(RAW * turn + r, r)

            def load_fin_x(n):
                wait(sp, w_lo_done, 3 * NI) if isinstance(n, int) else sp.wait_ge(fin_stored, 16 * J * n)
                src = x_blocks[bass.ds(n, 1)].rearrange("a p j e -> (a p) j e")
                sp.dma_start(fin, src).then_inc(fin_x_loaded, 16)

            def store(n):
                dst = out_tiles[bass.ds(n, 1)].rearrange("a p j e -> (a p) j e")
                for j in range(J):
                    sp.wait_ge(fin_done, J * n + j + 1)
                    sp.dma_start(dst[:, j, :], fin[:, j, :]).then_inc(fin_stored, 16)

            load_fin_x(0)
            store(0)
            with sp.Fori(1, NB) as n:
                load_fin_x(n)
                store(n)
            sp.wait_ge(fin_stored, 16 * TILES)

        @block.gpsimd
        def _(pool):
            pool.memset(ident[:], 0.0).then_inc(ident_zero, 1)
            pool.memset(half[:], 0.5).then_inc(const_done, 1)
            pool.memset(minus_half[:], -0.5).then_inc(const_done, 1)
            pool.wait_ge(ident_zero, 1)
            pool.affine_select(out=ident[:], in_=ident[:], compare_op=ALU.not_equal, fill=1.0, base=0,
                               pattern=[[-1, P]], channel_multiplier=1).then_inc(const_done, 1)
            pool.wait_ge(const_done, 3)

            def scales(blk, source):
                if isinstance(blk, int) and blk == 0:
                    for j in range(J):
                        pool.wait_ge(var_done, j + 1)
                        t = slice(j, j + 1)
                        pool.tensor_tensor(z_scale[:, t], z_var[:, t], minus_half[:, t], ALU.pow)\
                            .then_inc(z_scale_done, 1)
                    pool.wait_ge(var_done, J + 1)
                else:
                    pool.wait_ge(var_done, (J + 1) * (blk + 1))
                    pool.tensor_tensor(z_scale[:], z_var[:], minus_half[:], ALU.pow).then_inc(z_scale_done, J)
                pool.tensor_tensor(x_rstd[:], x_var[:], minus_half[:], ALU.pow).then_inc(pool_step, 1)
                pool.tensor_tensor(z_std[:], z_var[:], half[:], ALU.pow).then_inc(pool_step, 1)
                pool.wait_ge(pool_step, 2 * (blk + 1))
                pool.tensor_tensor(rms[:, bass.ds(source * J, J)], x_rstd[:], z_std[:], ALU.mult)\
                    .then_inc(rms_done, 1)

            def next_x(blk, source):
                pool.wait_ge(transposed, J * (blk + 1))
                src = x_blocks[bass.ds(source, 1)].rearrange("a p j e -> (a p) j e")
                pool.dma_start(z[:], src).then_inc(x_loaded, 16)

            def keep_zT(blk):
                pool.wait_ge(zT_raw_done, J * blk)
                dst = zT_kept[bass.ds(blk - 1, 1)].rearrange("a p n -> (a p) n")
                pool.dma_start(dst, zT_raw[:].rearrange("p k t -> p (k t)")).then_inc(zT_stored, 16)

            scales(0, 0)
            next_x(0, 1)
            scales(1, 1)
            with pool.Fori(1, NB - 1) as blk:
                next_x(blk, blk + 1)
                keep_zT(blk)
                scales(blk + 1, blk + 1)
            next_x(NB - 1, 0)
            keep_zT(NB - 1)
            scales(NB, 0)
            pool.wait_ge(zT_stored, 16 * (NB - 1))
            with pool.Fori(NB, LAST) as blk:
                pool.wait_ge(zT_lo_done, K * (blk + 1))
                src = zT_kept[bass.ds(blk - NB, 1)].rearrange("a p n -> (a p) n")
                pool.dma_start(zT_raw[:].rearrange("p k t -> p (k t)"), src).then_inc(zT_loaded, 16)

        @block.tensor
        def _(pe):
            def product(acc, pairs, start, stop):
                for n, (lhsT, rhs) in enumerate(pairs):
                    last = pe.matmul(acc, lhsT, rhs, start=start and n == 0,
                                     stop=stop and n == len(pairs) - 1)
                return last

            def expand(w_hi, w_lo, step):
                pairs = []
                for k in range(K):
                    pairs += [(w_hi[:, step, k, :], zT_hi[:, k, :]), (w_hi[:, step, k, :], zT_lo[:, k, :]),
                              (w_lo[:, step, k, :], zT_hi[:, k, :])]
                return pairs

            def first_gate_product(blk, phase, first):
                pairs = expand(gate_hi, gate_lo, 0)
                wait(pe, silu_done, S * blk)
                pe.wait_ge(w_hi_done, 3 * S * phase + 1)
                pe.wait_ge(zT_hi_done, K * (blk + 1))
                product(gate_ps[:], pairs[0::3], True, False)
                if first:
                    pe.wait_ge(w_lo_done, 1)
                    product(gate_ps[:], pairs[2::3], False, False)
                    pe.wait_ge(zT_lo_done, K)
                    product(gate_ps[:], pairs[1::3], False, True).then_inc(gate_done, 1)
                else:
                    pe.wait_ge(zT_lo_done, K * (blk + 1))
                    product(gate_ps[:], pairs[1::3], False, False)
                    pe.wait_ge(w_lo_done, 3 * S * phase + 1)
                    product(gate_ps[:], pairs[2::3], False, True).then_inc(gate_done, 1)

            def gate_product(blk, phase, i):
                pe.wait_ge(w_lo_done, 3 * (S * phase + i) + 1)
                pe.wait_ge(silu_done, S * blk + i)
                product(gate_ps[:], expand(gate_hi, gate_lo, i), True, True).then_inc(gate_done, 1)

            def up_product(blk, phase, i):
                pe.wait_ge(w_lo_done, 3 * (S * phase + i) + 2)
                wait(pe, h_done, slot_free(blk, i))
                product(up_ps[:, i % 2, :], expand(up_hi, up_lo, i), True, True).then_inc(up_done, 1)

            def down_wait(blk, phase, i):
                pe.wait_ge(w_lo_done, 3 * (S * phase + i) + 3)
                pe.wait_ge(h_lo_done, S * blk + i + 1)
                if i == 0:
                    wait(pe, y_free, J * blk)

            def down_tile(i, j):
                t = slice(j * P, (j + 1) * P)
                pairs = [(h_hi[:, i % 2, t], down_hi[:, i, :]), (h_hi[:, i % 2, t], down_lo[:, i, :]),
                         (h_lo[:, i % 2, t], down_hi[:, i, :])]
                product(y_ps[:, j, :], pairs, i == 0, i == S - 1).then_inc(down_done, 1)

            def down_product(blk, phase, i):
                down_wait(blk, phase, i)
                for j in range(J):
                    down_tile(i, j)

            def qkv_product(blk, phase, a):
                if isinstance(blk, int) and blk == 0 and a == 0:
                    pe.wait_ge(wqkv_lo_done, 1)
                if a:
                    pe.wait_ge(qkv_in_sbuf, A * blk + a)
                t = slice((A * phase + a) * P, (A * phase + a + 1) * P)
                pairs = []
                for k in range(K):
                    pairs += [(zT_hi[:, k, t], wqkv_hi[:, k, :]), (zT_hi[:, k, t], wqkv_lo[:, k, :]),
                              (zT_lo[:, k, t], wqkv_hi[:, k, :])]
                product(aux_ps[:, 0:QKV], pairs, True, True).then_inc(qkv_done, 1)

            def transpose_tile(dst, blk, j):
                pe.wait_ge(z_done, J * blk + j + 1)
                for k in range(K):
                    last = pe.transpose(dst[:, k * P:(k + 1) * P], z[:, j, k * P:(k + 1) * P], ident[:])
                last.then_inc(transposed, 1)

            def transpose_next(blk, j):
                if j:
                    pe.wait_ge(zT_raw_done, J * blk + j)
                else:
                    pe.wait_ge(qkv_in_sbuf, A * (blk + 1))
                transpose_tile(aux_ps, blk + 1, j)

            def one_block(blk, phase, first=False, last=False):
                for i in range(S):
                    if i == 0:
                        first_gate_product(blk, phase, first)
                    else:
                        gate_product(blk, phase, i)
                    if i == S - 1 and phase == 0:
                        transpose_next(blk, J - 1)
                    up_product(blk, phase, i)
                    if first and i == QKV_STEP:
                        down_product(blk, phase, i - 1)
                    if QKV_STEP <= i < TRANSPOSE_STEP:
                        qkv_product(blk, phase, i - QKV_STEP)
                    if TRANSPOSE_STEP <= i < S - 1 and phase == 0:
                        transpose_next(blk, i - TRANSPOSE_STEP)
                    if i and not (last and i == S - 1) and not (first and i == QKV_STEP):
                        down_product(blk, phase, i - 1)
                if not last:
                    down_product(blk, phase, S - 1)
                else:
                    down_wait(blk, phase, S - 2)
                    for j in range(J - 1):
                        down_tile(S - 2, j)
                    down_wait(blk, phase, S - 1)
                    for j in range(J - 1):
                        down_tile(S - 1, j)
                    down_tile(S - 2, J - 1)
                    down_tile(S - 1, J - 1)

            pe.wait_ge(const_done, 3)
            for n in range(WARM_UP):
                pe.transpose(aux_ps[:, 0:P], ident[:], ident[:])
            for j in range(J):
                transpose_tile(y_ps[:, j, :], 0, j)
            one_block(0, 0, first=True)
            with pe.Fori(1, NB) as blk:
                one_block(blk, 0)
            with pe.Fori(NB, LAST) as blk:
                one_block(blk, 1)
            one_block(LAST, 1, last=True)

        @block.scalar
        def _(act):
            def arrived(step, n):
                act.wait_ge(raw_loaded[3 * (step % RAW) + n], 16 * (step // RAW + 1))

            def scale_weights(step, n):
                arrived(step, n)
                for k in range(K):
                    part = raw[:, 3 * (step % RAW) + n, k * P:(k + 1) * P]
                    last = act.activation(part, part, ACT.Copy, scale=lnw_sb[:, k:k + 1])
                last.then_inc(w_scaled, 1)

            def weights_hi(phase, i, pieces=range(3), scaled=False):
                step = S * phase + i
                for n in pieces:
                    if n < 2:
                        if not scaled:
                            scale_weights(step, n)
                        act.wait_ge(w_scaled, 2 * step + n + 1)
                        w_hi = (gate_hi, up_hi)[n][:, i, :, :].rearrange("p k n -> p (k n)")
                    else:
                        arrived(step, n)
                        w_hi = down_hi[:, i, :]
                    act.activation(w_hi, raw[:, 3 * (step % RAW) + n, :], ACT.Copy).then_inc(w_hi_done, 1)

            def zT_raw_tile(blk, j):
                act.wait_ge(transposed, J * blk + j + 1)
                if j == 0:
                    act.wait_ge(zT_lo_done, K * blk)
                    wait(act, zT_stored, 16 * (blk - 1))
                act.activation(zT_raw[:, :, j * P:(j + 1) * P], aux_ps[:].rearrange("p (k t) -> p k t", k=K),
                               ACT.Copy).then_inc(zT_raw_done, 1)

            def zT_hi_chunk(k):
                act.activation(zT_hi[:, k, :], zT_raw[:, k, :], ACT.Copy).then_inc(zT_hi_done, 1)

            def h_hi_part(blk, i):
                act.wait_ge(h_done, S * blk + i + 1)
                wait(act, down_done, J * slot_free(blk, i))
                act.activation(h_hi[:, i % 2, :], h[:, i % 2, :], ACT.Copy).then_inc(h_hi_done, 1)

            def one_block(blk, phase, first=False, last=False, before=None):
                for i in range(S):
                    early = phase and i + 1 < RAW
                    if first and i + 1 < S:
                        weights_hi(phase, i + 1, (0,), early)
                    wait(act, h_lo_done, slot_free(blk, i))
                    act.wait_ge(gate_done, S * blk + i + 1)
                    act.activation(h[:, i % 2, :], gate_ps[:], ACT.Silu).then_inc(silu_done, 1)
                    if first and i + 1 < S:
                        weights_hi(phase, i + 1, (1, 2), early)
                    if i == 0 and before == 0:
                        for j in range(J):
                            act.wait_ge(down_done, y_whole(blk - 1, j))
                            act.activation(y_part[:, bass.ds((J * blk - J + j) * E, E)], y_ps[:, j, :],
                                           ACT.Copy).then_inc(y_free, 1)
                    if i < S - 1 or last:
                        h_hi_part(blk, i)
                    else:
                        if phase == 0:
                            zT_raw_tile(blk + 1, J - 1)
                            act.wait_ge(zT_raw_done, J * (blk + 1))
                        else:
                            act.wait_ge(zT_loaded, 16 * (blk + 1 - NB))
                        act.wait_ge(up_done, S * (blk + 1))
                        zT_hi_chunk(0)
                        h_hi_part(blk, i)
                        for k in range(1, K):
                            zT_hi_chunk(k)
                    if i == 0 and before is None:
                        act.wait_ge(wqkv_summed, K)
                        act.wait_ge(qkv_w_loaded, 48)
                        act.activation(wqkv_hi[:], wqkv_raw, ACT.Copy).then_inc(wqkv_hi_done, 1)
                    if i == 0 and before == 1:
                        y_gate(blk)
                    if TRANSPOSE_STEP <= i < S - 1 and phase == 0:
                        zT_raw_tile(blk + 1, i - TRANSPOSE_STEP)
                    if i == EXP_STEP[last]:
                        act.wait_ge(attn_step, ATT * blk + 6 * A)
                        act.activation(scores[:], scores[:], ACT.Exp, scale=float(D) ** -0.5).then_inc(exp_done, 1)

            def y_gate(blk):
                for j in range(J):
                    act.wait_ge(y_free, J * (blk - 1) + j + 1)
                    y = y_part[:, bass.ds((J * (blk - 1 - NB) + j) * E, E)]
                    act.activation(y, y, ACT.Silu).then_inc(y_gate_done, 1)

            act.wait_ge(table_loaded, 1)
            act.activation(scratch[:, 1:2], scratch[:, 0:1], ACT.Silu).then_inc(table_loaded, 1)
            act.wait_ge(lnw_loaded, 16)
            weights_hi(0, 0, (0,))
            for j in range(J):
                act.wait_ge(transposed, j + 1)
                act.activation(zT_hi[:, :, j * P:(j + 1) * P], y_ps[:, j, :].rearrange("p (k t) -> p k t", k=K),
                               ACT.Copy).then_inc(zT_hi_done, 1)
            weights_hi(0, 0, (1, 2))
            one_block(0, 0, first=True)
            for step in range(S, S + RAW):
                scale_weights(step, 0)
                scale_weights(step, 1)
            with act.Fori(1, NB) as blk:
                one_block(blk, 0, before=0)
            act.wait_ge(down_done, J * (S * (NB - 1) + 1))
            weights_hi(1, 0, scaled=True)
            one_block(NB, 1, first=True, before=0)
            with act.Fori(NB + 1, LAST) as blk:
                one_block(blk, 1, before=1)
            one_block(LAST, 1, last=True, before=1)
            y_gate(LAST + 1)

        @block.vector
        def _(dve):
            def weights_lo(phase, i, pieces=range(3)):
                step = S * phase + i
                for n in pieces:
                    slot = 3 * (step % RAW) + n
                    w_hi, w_lo = ((gate_hi, gate_lo), (up_hi, up_lo), (down_hi, down_lo))[n]
                    w_hi, w_lo = w_hi[:, i], w_lo[:, i]
                    if n < 2:
                        w_hi, w_lo = w_hi.rearrange("p k n -> p (k n)"), w_lo.rearrange("p k n -> p (k n)")
                    dve.wait_ge(w_hi_done, 3 * step + n + 1)
                    dve.tensor_tensor(w_lo, raw[:, slot, :], w_hi.bitcast(F32), ALU.subtract)\
                        .then_inc(w_lo_done, 1)

            def statistics(blk):
                dve.wait_ge(x_loaded, 16 * blk)
                for j in range(J):
                    dve.bn_stats(stats[:, j, :], z[:, j, :]).then_inc(bn_done, 1)
                dve.wait_ge(bn_done, J * (blk + 1))
                dve.memset(scratch[:, 2:3], 0.0)
                for j in range(J):
                    dve.bn_aggr(mean_var[:, j, :], stats[:, j, :]).then_inc(stats_done, 1)
                dve.wait_ge(rms_done, blk)
                dve.wait_ge(stats_done, J * (blk + 1))
                dve.tensor_scalar(z_var[:], mean_var[:, :, 1], 1.0 + EPS, EPS * EPS, ALU.mult, ALU.add)\
                    .then_inc(var_done, J)
                dve.tensor_scalar(x_var[:], mean_var[:, :, 1], EPS, None, ALU.add).then_inc(var_done, 1)

            def normalise_tile(j):
                dve.tensor_scalar(z[:, j, :], z[:, j, :], mean_var[:, j, 0:1], z_scale[:, j:j + 1],
                                  ALU.subtract, ALU.mult).then_inc(z_done, 1)

            def normalise(blk):
                dve.wait_ge(z_scale_done, J * (blk + 1))
                for j in range(J):
                    normalise_tile(j)

            def first_block():
                def variance(j):
                    dve.wait_ge(bn_done, j + 1)
                    dve.bn_aggr(mean_var[:, j, :], stats[:, j, :]).then_inc(stats_done, 1)
                    dve.wait_ge(stats_done, j + 1)
                    dve.tensor_scalar(z_var[:, j:j + 1], mean_var[:, j, 1:2], 1.0 + EPS, EPS * EPS,
                                      ALU.mult, ALU.add).then_inc(var_done, 1)

                for j in range(J):
                    dve.wait_ge(x_first[j], 16)
                    dve.bn_stats(stats[:, j, :], z[:, j, :]).then_inc(bn_done, 1)
                    if j:
                        variance(j - 1)
                    if j > 1:
                        dve.wait_ge(z_scale_done, j - 1)
                        normalise_tile(j - 2)
                variance(J - 1)
                dve.wait_ge(z_scale_done, J - 1)
                normalise_tile(J - 2)
                dve.tensor_scalar(x_var[:], mean_var[:, :, 1], EPS, None, ALU.add).then_inc(var_done, 1)
                dve.wait_ge(z_scale_done, J)
                normalise_tile(J - 1)
                weights_lo(0, 0, (0,))

            def zT_lo_chunk(blk, k):
                dve.wait_ge(zT_hi_done, K * blk + k + 1)
                dve.tensor_tensor(zT_lo[:, k, :], zT_raw[:, k, :], zT_hi[:, k, :].bitcast(F32),
                                  ALU.subtract).then_inc(zT_lo_done, 1)

            def qkv_out(blk, tile, a):
                dve.wait_ge(qkv_done, A * blk + a + 1)
                dve.scalar_tensor_tensor(qkv[:, a, :], aux_ps[:, 0:QKV], rms[:, bass.ds(tile, 1)], bias[:],
                                         ALU.mult, ALU.add).then_inc(qkv_in_sbuf, 1)

            def attn_chain(blk, start):
                count = [ATT * blk + start]

                def step(instruction):
                    count[0] = count[0] + 1
                    instruction.then_inc(attn_step, 1)
                    dve.wait_ge(attn_step, count[0])
                return step

            def attn_scores(blk, a, parts=(0, 1, 2)):
                step = attn_chain(blk, 6 * a + 2 * parts[0])
                dve.wait_ge(qkv_in_sbuf, A * blk + a + 1)
                q = qkv[:, a, 0:DG].rearrange("p (d g) -> p d g", g=HKV)
                k = qkv[:, a, DG:2 * DG].rearrange("p (e g) -> p e g", g=HKV)
                pr = prod[:].rearrange("p (d e g) -> p d e g", e=D, g=HKV)
                s = scores[:, a, :].rearrange("p (d e) -> p d e", e=D)
                for d in [HALF * part for part in parts if part < 2]:
                    step(dve.tensor_tensor(pr, q[:, d:d + HALF, :].unsqueeze(2).to_broadcast([P, HALF, D, HKV]),
                                           k.unsqueeze(1).to_broadcast([P, HALF, D, HKV]), ALU.mult))
                    step(dve.tensor_reduce(s[:, d:d + HALF, :], pr, X, ALU.add))
                if 2 in parts:
                    step(dve.tensor_reduce(row_max[:, a, :], s, X, ALU.max))
                    step(dve.tensor_tensor(s, s, row_max[:, a, :].unsqueeze(2).to_broadcast([P, D, D]), ALU.subtract))

            def attn_values(blk, tile, a, parts=(0, 1, 2)):
                step = attn_chain(blk, 6 * A + 7 * a + 2 * parts[0])
                dve.wait_ge(exp_done, blk + 1)
                e = scores[:, a, :].rearrange("p (d e) -> p d e", e=D)
                v = qkv[:, a, 2 * DG:].rearrange("p (g e) -> p g e", e=D)
                pr = prod[:].rearrange("p (d g e) -> p d g e", g=HKV, e=D)
                o = attn[:, bass.ds(tile * DG, DG)].rearrange("p (d g) -> p d g", g=HKV)
                for d in [HALF * part for part in parts if part < 2]:
                    step(dve.tensor_tensor(pr, e[:, d:d + HALF, :].unsqueeze(2).to_broadcast([P, HALF, HKV, D]),
                                           v.unsqueeze(1).to_broadcast([P, HALF, HKV, D]), ALU.mult))
                    step(dve.tensor_reduce(o[:, d:d + HALF, :], pr, X, ALU.add))
                if 2 in parts:
                    step(dve.tensor_reduce(row_sum[:, a, :], e, X, ALU.add))
                    step(dve.reciprocal(row_inv[:, a, :], row_sum[:, a, :]))
                    step(dve.tensor_tensor(o, o, row_inv[:, a, :].unsqueeze(2).to_broadcast([P, D, HKV]), ALU.mult))

            def y_sum(blk, tiles=range(J)):
                for j in tiles:
                    dve.wait_ge(down_done, y_whole(blk - 1, j))
                    y = y_part[:, bass.ds((J * (blk - 1 - NB) + j) * E, E)]
                    dve.tensor_tensor(y, y_ps[:, j, :], y, ALU.add).then_inc(y_free, 1)

            def finish(blk, j):
                n = blk - 1 - NB
                tile = J * n + j
                y = y_part[:, bass.ds(tile * E, E)]
                s = attn[:, bass.ds(tile * DG, DG)].unsqueeze(2).to_broadcast([P, DG, REP])
                y3 = y.rearrange("p (s r) -> p s r", r=REP)
                dve.wait_ge(y_gate_done, tile + 1)
                dve.tensor_tensor(y3, y3, s, ALU.mult).then_inc(gated_done, 1)
                if j == 0:
                    dve.wait_ge(fin_x_loaded, 16 * (n + 1))
                dve.wait_ge(gated_done, tile + 1)
                dve.tensor_tensor(fin[:, j, :], y, fin[:, j, :], ALU.add).then_inc(fin_done, 1)

            def sum_wq(chunks):
                dve.wait_ge(qkv_w_loaded, 48)
                for k in chunks:
                    dve.tensor_reduce(wqkv_raw[:, k, 0:DG], wq_raw[:, k, :].rearrange("p (n r) -> p n r", r=REP),
                                      X, ALU.add).then_inc(wqkv_summed, 1)

            def qkv_weights_lo():
                dve.wait_ge(bias_loaded, 48)
                dve.tensor_reduce(bias[:, 0:DG], bq_raw.rearrange("p (n r) -> p n r", r=REP), X,
                                  ALU.add).then_inc(bias_summed, 1)
                dve.wait_ge(wqkv_hi_done, 1)
                dve.tensor_tensor(wqkv_lo[:], wqkv_raw, wqkv_hi[:].bitcast(F32), ALU.subtract)\
                   .then_inc(wqkv_lo_done, 1)
                dve.wait_ge(bias_summed, 1)

            def one_block(blk, phase, first=False, last=False, before=None):
                if before == 1:
                    y_sum(blk)
                for i in range(S):
                    if first and i + 1 < S and i + 1 not in (2, 3):
                        weights_lo(phase, i + 1, (0,))
                    if i == 0 and before is None:
                        sum_wq(range(K // 2))
                    dve.wait_ge(silu_done, S * blk + i + 1)
                    dve.wait_ge(up_done, S * blk + i + 1)
                    dve.tensor_tensor(h[:, i % 2, :], h[:, i % 2, :], up_ps[:, i % 2, :], ALU.mult)\
                       .then_inc(h_done, 1)
                    if first and i + 1 < S:
                        weights_lo(phase, i + 1, (1,))
                    if i == 0 and before is None:
                        sum_wq(range(K // 2, K))
                    dve.wait_ge(h_hi_done, S * blk + i + 1)
                    dve.tensor_tensor(h_lo[:, i % 2, :], h[:, i % 2, :], h_hi[:, i % 2, :].bitcast(F32),
                                      ALU.subtract).then_inc(h_lo_done, 1)
                    if first and i + 1 < S:
                        weights_lo(phase, i + 1, (2,))
                    tile = J * (blk - NB * phase) + A * phase
                    if i == 0 and before is None:
                        qkv_weights_lo()
                    elif i == 0:
                        former = J * (blk - 1 - NB * before) + A * before + 1
                        attn_values(blk - 1, former, 1, (0, 1))
                    if i == 0 and first:
                        weights_lo(phase, 2, (0,))
                    if i == 0 and before is not None:
                        attn_values(blk - 1, former, 1, (2,))
                    if i == 0 and phase == 0:
                        statistics(blk + 1)
                    if i == 1:
                        if phase == 0 or first:
                            dve.wait_ge(rms_done, blk + 1)
                        qkv_out(blk, tile, 0)
                        attn_scores(blk, 0, (0,))
                        if first:
                            weights_lo(phase, 3, (0,))
                        attn_scores(blk, 0, (1, 2))
                    if i == 2:
                        qkv_out(blk, tile + 1, 1)
                        if phase == 0:
                            normalise(blk + 1)
                    if i == SCORES_STEP[last]:
                        attn_scores(blk, 1)
                    if i in FINISH_STEPS and before == 1 and not last:
                        for j in range(J):
                            if FINISH_STEPS[j // 2] == i:
                                finish(blk, j)
                    if i == 3 and last:
                        for j in range(J):
                            finish(blk, j)
                    if i == VALUES_STEP:
                        attn_values(blk, tile, 0, (0,) if first else (0, 1, 2))
                    if i == VALUES_STEP + 1 and first:
                        attn_values(blk, tile, 0, (1, 2))
                    if i == S - 2 and last:
                        attn_values(blk, tile + 1, 1, (0, 1))
                    if i == S - 1 and last:
                        attn_values(blk, tile + 1, 1, (2,))
                if not last:
                    for k in range(K):
                        zT_lo_chunk(blk + 1, k)

            dve.memset(scratch[:, 0:1], 0.0).then_inc(table_loaded, 1)
            first_block()
            for j in range(J):
                dve.wait_ge(zT_hi_done, j + 1)
                t = slice(j * P, (j + 1) * P)
                dve.tensor_tensor(zT_lo[:, :, t], y_ps[:, j, :].rearrange("p (k t) -> p k t", k=K),
                                  zT_hi[:, :, t].bitcast(F32), ALU.subtract).then_inc(zT_lo_done, 1)
            weights_lo(0, 0, (1, 2))
            one_block(0, 0, first=True)
            with dve.Fori(1, NB) as blk:
                one_block(blk, 0, before=0)
            weights_lo(1, 0)
            one_block(NB, 1, first=True, before=0)
            with dve.Fori(NB + 1, LAST) as blk:
                one_block(blk, 1, before=1)
            one_block(LAST, 1, last=True, before=1)
            y_sum(LAST + 1, (0, 1))
            for j in range(J):
                finish(LAST + 1, j)
                if j + 2 < J:
                    y_sum(LAST + 1, (j + 2,))


def kernel(L0_attn_x, L0_attn_Wq, L0_attn_bq, L0_attn_Wk, L0_attn_bk, L0_attn_Wv, L0_attn_bv,
           L0_ffn_ln_w, L0_ffn_gate_w, L0_ffn_up_w, L0_ffn_down_w):
    import numpy as np
    import concourse.bacc as bacc
    from concourse.bass_utils import run_bass_kernel_spmd

    _, T, E = L0_attn_x.shape
    I = L0_ffn_gate_w.shape[0]

    def expand(w):
        return np.asarray(w).reshape(I // P, P, E // P, P).transpose(0, 3, 2, 1).reshape(I // P, P, E)

    arrays = {
        "x": np.asarray(L0_attn_x).reshape(T, E),
        "wq": np.asarray(L0_attn_Wq).reshape(E, -1),
        "bq": np.asarray(L0_attn_bq).reshape(-1),
        "wk": np.asarray(L0_attn_Wk).reshape(E, -1),
        "bk": np.asarray(L0_attn_bk).reshape(-1),
        "wv": np.asarray(L0_attn_Wv).transpose(0, 2, 1).reshape(E, -1),
        "bv": np.asarray(L0_attn_bv).T.reshape(-1),
        "lnw": np.asarray(L0_ffn_ln_w).reshape(E // P, P).T,
        "gate": expand(L0_ffn_gate_w),
        "up": expand(L0_ffn_up_w),
        "down": np.asarray(L0_ffn_down_w).T.reshape(I // P, P, E),
    }
    arrays = {name: np.ascontiguousarray(a) for name, a in arrays.items()}
    nc = bacc.Bacc("TRN2", target_bir_lowering=False, num_devices=1)
    args = [nc.dram_tensor(name, a.shape, mybir.dt.from_np(a.dtype), kind="ExternalInput").ap()
            for name, a in arrays.items()]
    out = nc.dram_tensor("out", (T, E), F32, kind="ExternalOutput").ap()
    build(nc, *args, out)
    r = run_bass_kernel_spmd(nc, [arrays], core_ids=[0])
    return np.asarray(r.results[0]["out"]).reshape(1, T, E)
```
